# Optimizing a Trainium2 kernel written in Bass

```python
import numpy as np
import jax
import jax.numpy as jnp

def _softmax(x, axis=-1):
    return jax.nn.softmax(x, axis=axis)

def _gelu(x):
    return jax.nn.gelu(x, approximate=True)

def _silu(x):
    return jax.nn.silu(x)

def _sigmoid(x):
    return jax.nn.sigmoid(x)

def _layernorm(x, axis=-1, eps=1e-05):
    m = jnp.mean(x, axis=axis, keepdims=True)
    v = jnp.var(x, axis=axis, keepdims=True)
    return (x - m) / jnp.sqrt(v + eps)

def _scatter_add(tgt, idx, src, axis=0):
    return tgt.at[idx].add(src)

def _segment_sum(src, seg, n):
    return jax.ops.segment_sum(src, seg, n)
kernel_name = 'mk_decoder_preln_d2_seqx_r8_b347c3'

def setup_inputs(seed: int=0):
    np.random.seed(seed)
    _w = jnp.asarray

    def _rec_inputs():
        import jax
        import jax.numpy as jnp
        _rk = jax.random.key(seed)
        x = 0.0003765 + 1 * jax.random.normal(jax.random.fold_in(_rk, 1), (16, 128, 256), jnp.float32)
        _lenS = 128 - jax.random.randint(jax.random.fold_in(_rk, 7), (16,), 0, max(1, 128 // 4) + 1, jnp.int32)
        _lenS2 = 128 - jax.random.randint(jax.random.fold_in(_rk, 8), (16,), 0, max(1, 128 // 4) + 1, jnp.int32)
        _ctx_2048P = jax.random.normal(jax.random.fold_in(_rk, 11), (16, 16, 256), jnp.float32)
        _ctx_2048c = jax.random.dirichlet(jax.random.fold_in(_rk, 511), 0.3 * jnp.ones((16,), jnp.float32), (16, 128))
        _ctx_2048t = jnp.einsum('bsk,bkd->bsd', _ctx_2048c, _ctx_2048P)
        _ctx_2048t = _ctx_2048t * jax.lax.rsqrt(jnp.mean(jnp.square(_ctx_2048t)) + 1e-12) * 0.953939
        ctx_2048 = -0.000292821 + 1.00034 * (_ctx_2048t + 0.3 * jax.random.normal(jax.random.fold_in(_rk, 611), (16, 128, 256), jnp.float32))
        _validS = jnp.arange(128)[None, :] < _lenS[:, None]
        _validS2 = jnp.arange(128)[None, :] < _lenS2[:, None]
        _causal = jnp.tril(jnp.ones((128, 128), dtype=bool))
        mask_BxS2_bk0 = jnp.logical_not(jnp.broadcast_to(_validS2[:, :], (16, 128)))
        return (x, ctx_2048, mask_BxS2_bk0)
    x, ctx_2048, mask_BxS2_bk0 = _rec_inputs()

    def _L0_attn_setup():
        import jax, jax.numpy as jnp
        import numpy as np
        import math
        EMBED_DIM = 256
        NUM_HEADS = 16
        HEAD_DIM = EMBED_DIM // NUM_HEADS
        BATCH = 4
        SEQ = 256
        key = jax.random.key(seed)
        ks = jax.random.split(key, 5)
        scale_qkv = 1.0 / math.sqrt(EMBED_DIM)
        x = jax.random.normal(ks[0], (BATCH, SEQ, EMBED_DIM), dtype=jnp.float32)
        w_qkv = jax.random.normal(ks[1], (3 * EMBED_DIM, EMBED_DIM), dtype=jnp.float32) * scale_qkv
        b_qkv = jnp.zeros((3 * EMBED_DIM,), dtype=jnp.float32)
        w_o = jax.random.normal(ks[2], (EMBED_DIM, EMBED_DIM), dtype=jnp.float32) * scale_qkv
        b_o = jnp.zeros((EMBED_DIM,), dtype=jnp.float32)
        return {'x': x, 'w_qkv': w_qkv, 'b_qkv': b_qkv, 'w_o': w_o, 'b_o': b_o}
    _L0_attn_all = _L0_attn_setup()
    _L0_attn_in = {k: v for k, v in _L0_attn_all.items() if k in ('w_qkv', 'b_qkv', 'w_o', 'b_o')}
    del _L0_attn_all

    def _L0_xattn_setup():
        import jax, jax.numpy as jnp
        import numpy as np
        key = jax.random.key(seed)
        k1, k2, k3, k4, k5 = jax.random.split(key, 5)
        B, D_MODEL, L = (2, 128, 256)
        HEAD_DIM = 8
        H = D_MODEL // HEAD_DIM
        return {'k': jax.random.normal(k1, (B, D_MODEL, L), dtype=jnp.float32), 'v': jax.random.normal(k2, (B, D_MODEL, L), dtype=jnp.float32), 'q': jax.random.normal(k3, (B, D_MODEL, L), dtype=jnp.float32), 'ssm_kernel': jax.random.normal(k4, (H, L), dtype=jnp.float32), 'D': jax.random.normal(k5, (H,), dtype=jnp.float32), 'head_dim': HEAD_DIM}
    _L0_xattn_all = _L0_xattn_setup()
    _L0_xattn_in = {k: v for k, v in _L0_xattn_all.items() if k in ('ssm_kernel', 'D')}
    del _L0_xattn_all

    def _L0_ffn_setup():
        import jax, jax.numpy as jnp
        import numpy as np

        def _glu(x, wg, wu, wd):
            return jax.nn.silu(x @ wg) * (x @ wu) @ wd
        key = jax.random.key(seed)
        ks = jax.random.split(key, 8)
        B, S, H, I, E = (4, 256, 256, 256, 8)
        s = 0.02
        return {'hidden_states': jax.random.normal(ks[0], (B, S, H), jnp.float32), 'router_w': jax.random.normal(ks[1], (E, H), jnp.float32) * s, 'w1': jax.random.normal(ks[2], (E, H, I), jnp.float32) * s, 'v1': jax.random.normal(ks[3], (E, H, I), jnp.float32) * s, 'w2': jax.random.normal(ks[4], (E, I, H), jnp.float32) * s, 'shared_gate': jax.random.normal(ks[5], (I, H), jnp.float32) * s, 'shared_up': jax.random.normal(ks[6], (I, H), jnp.float32) * s, 'shared_down': jax.random.normal(ks[7], (H, I), jnp.float32) * s}
    _L0_ffn_all = _L0_ffn_setup()
    _L0_ffn_in = {k: v for k, v in _L0_ffn_all.items() if k in ('router_w', 'w1', 'v1', 'w2', 'shared_gate', 'shared_up', 'shared_down')}
    del _L0_ffn_all

    def _L1_attn_setup():
        import jax, jax.numpy as jnp
        import numpy as np
        import math
        HIDDEN = 256
        NUM_HEADS = 16
        HEAD_DIM = HIDDEN // NUM_HEADS
        BATCH = 2
        SEQ = 512
        BLOCK = 128
        TOPK = 64
        NEG = -1000000000.0

        def _split_heads(x):
            n, t, _ = x.shape
            return x.reshape(n, t, NUM_HEADS, HEAD_DIM).transpose(0, 2, 1, 3)

        def _local_attention(q, k, v):
            n, h, t, d = q.shape
            nb = t // BLOCK
            half = BLOCK // 2
            qb = q.reshape(n, h, nb, BLOCK, d)
            win = jnp.arange(nb)[:, None] * BLOCK - half + jnp.arange(2 * BLOCK)[None, :]
            valid = (win >= 0) & (win < t)
            winc = jnp.clip(win, 0, t - 1)
            kb = k[:, :, winc, :]
            vb = v[:, :, winc, :]
            scores = jnp.einsum('nhbqd,nhbkd->nhbqk', qb, kb) / math.sqrt(d)
            scores = jnp.where(valid[None, None, :, None, :], scores, NEG)
            probs = jax.nn.softmax(scores, axis=-1)
            ctx = jnp.einsum('nhbqk,nhbkd->nhbqd', probs, vb)
            return ctx.reshape(n, h, t, d)

        def _global_index(q):
            n, h, t, d = q.shape
            norm = jnp.linalg.norm(q, axis=-1)
            _, top_idx = jax.lax.top_k(norm, TOPK - 2)
            bos = jnp.zeros((n, h, 1), jnp.int32)
            eos = jnp.full((n, h, 1), t - 1, jnp.int32)
            return jnp.concatenate([bos, top_idx.astype(jnp.int32), eos], axis=-1)
        key = jax.random.key(seed)
        ks = jax.random.split(key, 7)
        s = 1.0 / math.sqrt(HIDDEN)
        return {'hidden_states': jax.random.normal(ks[0], (BATCH, SEQ, HIDDEN), jnp.float32), 'Wq': jax.random.normal(ks[1], (HIDDEN, HIDDEN), jnp.float32) * s, 'bq': jnp.zeros((HIDDEN,), jnp.float32), 'Wk': jax.random.normal(ks[2], (HIDDEN, HIDDEN), jnp.float32) * s, 'bk': jnp.zeros((HIDDEN,), jnp.float32), 'Wv': jax.random.normal(ks[3], (HIDDEN, HIDDEN), jnp.float32) * s, 'bv': jnp.zeros((HIDDEN,), jnp.float32)}
    _L1_attn_all = _L1_attn_setup()
    _L1_attn_in = {k: v for k, v in _L1_attn_all.items() if k in ('Wq', 'bq', 'Wk', 'bk', 'Wv', 'bv')}
    del _L1_attn_all

    def _L1_xattn_setup():
        import jax, jax.numpy as jnp
        import numpy as np
        key = jax.random.key(seed)
        k1, k2, k3 = jax.random.split(key, 3)
        B, S, D, M = (8, 256, 256, 128)
        hidden_states = jax.random.normal(k1, (B, S, D), dtype=jnp.float32)
        memory_tokens = jax.random.normal(k2, (B, M, D), dtype=jnp.float32)
        memory_mask = jax.random.randint(k3, (B, M), 0, 2).astype(jnp.bool_)
        return {'hidden_states': hidden_states, 'memory_tokens': memory_tokens, 'memory_mask': memory_mask}
    _L1_xattn_all = _L1_xattn_setup()
    _L1_xattn_in = {k: v for k, v in _L1_xattn_all.items() if k in ()}
    del _L1_xattn_all

    def _L1_ffn_setup():
        import jax, jax.numpy as jnp
        import numpy as np
        EPS = 1e-05

        def rms_norm(x):
            return x * jax.lax.rsqrt(jnp.mean(x * x, axis=-1, keepdims=True) + EPS)

        def act_quant(x):
            scale = 127.0 / jnp.clip(jnp.max(jnp.abs(x), axis=-1, keepdims=True), 1e-05)
            q = jnp.clip(jnp.round(x * scale), -128.0, 127.0) / scale
            return x + jax.lax.stop_gradient(q - x)

        def weight_quant(w):
            scale = 1.0 / jnp.clip(jnp.mean(jnp.abs(w)), 1e-05)
            q = jnp.clip(jnp.round(w * scale), -1.0, 1.0) / scale
            return w + jax.lax.stop_gradient(q - w)

        def bitlinear158(x, w, b):
            xq = act_quant(rms_norm(x))
            wq = weight_quant(w)
            return jnp.einsum('bsd,od->bso', xq, wq) + b

        def layer_norm(x, g, b):
            mu = jnp.mean(x, axis=-1, keepdims=True)
            var = jnp.mean((x - mu) ** 2, axis=-1, keepdims=True)
            return (x - mu) * jax.lax.rsqrt(var + EPS) * g + b
        key = jax.random.key(seed)
        ks = jax.random.split(key, 3)
        d, inner = (256, 1024)
        x = jax.random.normal(ks[0], (4, 256, d), dtype=jnp.float32)
        w1 = jax.random.normal(ks[1], (inner, d), dtype=jnp.float32) * 0.02
        b1 = jnp.zeros((inner,), jnp.float32)
        ln_g = jnp.ones((inner,), jnp.float32)
        ln_b = jnp.zeros((inner,), jnp.float32)
        w2 = jax.random.normal(ks[2], (d, inner), dtype=jnp.float32) * 0.02
        b2 = jnp.zeros((d,), jnp.float32)
        return {'x': x, 'w1': w1, 'b1': b1, 'ln_g': ln_g, 'ln_b': ln_b, 'w2': w2, 'b2': b2}
    _L1_ffn_all = _L1_ffn_setup()
    _L1_ffn_in = {k: v for k, v in _L1_ffn_all.items() if k in ('w1', 'b1', 'ln_g', 'ln_b', 'w2', 'b2')}
    del _L1_ffn_all
    return {'x': x, 'ctx_2048': ctx_2048, 'mask_BxS2_bk0': mask_BxS2_bk0, 'L0_attn_w_qkv': _L0_attn_in['w_qkv'], 'L0_attn_b_qkv': _L0_attn_in['b_qkv'], 'L0_attn_w_o': _L0_attn_in['w_o'], 'L0_attn_b_o': _L0_attn_in['b_o'], 'L0_xattn_ssm_kernel': _L0_xattn_in['ssm_kernel'], 'L0_xattn_D': _L0_xattn_in['D'], 'L0_ffn_router_w': _L0_ffn_in['router_w'], 'L0_ffn_w1': _L0_ffn_in['w1'], 'L0_ffn_v1': _L0_ffn_in['v1'], 'L0_ffn_w2': _L0_ffn_in['w2'], 'L0_ffn_shared_gate': _L0_ffn_in['shared_gate'], 'L0_ffn_shared_up': _L0_ffn_in['shared_up'], 'L0_ffn_shared_down': _L0_ffn_in['shared_down'], 'L1_attn_Wq': _L1_attn_in['Wq'], 'L1_attn_bq': _L1_attn_in['bq'], 'L1_attn_Wk': _L1_attn_in['Wk'], 'L1_attn_bk': _L1_attn_in['bk'], 'L1_attn_Wv': _L1_attn_in['Wv'], 'L1_attn_bv': _L1_attn_in['bv'], 'L1_ffn_w1': _L1_ffn_in['w1'], 'L1_ffn_b1': _L1_ffn_in['b1'], 'L1_ffn_ln_g': _L1_ffn_in['ln_g'], 'L1_ffn_ln_b': _L1_ffn_in['ln_b'], 'L1_ffn_w2': _L1_ffn_in['w2'], 'L1_ffn_b2': _L1_ffn_in['b2']}

def reference(x, ctx_2048, mask_BxS2_bk0, L0_attn_w_qkv, L0_attn_b_qkv, L0_attn_w_o, L0_attn_b_o, L0_xattn_ssm_kernel, L0_xattn_D, L0_ffn_router_w, L0_ffn_w1, L0_ffn_v1, L0_ffn_w2, L0_ffn_shared_gate, L0_ffn_shared_up, L0_ffn_shared_down, L1_attn_Wq, L1_attn_bq, L1_attn_Wk, L1_attn_bk, L1_attn_Wv, L1_attn_bv, L1_ffn_w1, L1_ffn_b1, L1_ffn_ln_g, L1_ffn_ln_b, L1_ffn_w2, L1_ffn_b2):
    import jax
    import jax.numpy as jnp

    def _L0_attn_ref(x, w_qkv, b_qkv, w_o, b_o):
        import jax, jax.numpy as jnp
        import numpy as np
        import math
        EMBED_DIM = 256
        NUM_HEADS = 16
        HEAD_DIM = EMBED_DIM // NUM_HEADS
        BATCH = 4
        SEQ = 256
        B, S, D = x.shape
        qkv = jnp.einsum('bsd,ed->bse', x, w_qkv) + b_qkv
        qkv = qkv.reshape(B, S, 3, NUM_HEADS, HEAD_DIM)
        qkv = jnp.transpose(qkv, (2, 0, 3, 1, 4))
        q, k, v = (qkv[0], qkv[1], qkv[2])
        scores = jnp.einsum('bhqd,bhkd->bhqk', q, k) / math.sqrt(HEAD_DIM)
        probs = jax.nn.softmax(scores, axis=-1)
        out = jnp.einsum('bhqk,bhkd->bhqd', probs, v)
        out = jnp.transpose(out, (0, 2, 1, 3)).reshape(B, S, D)
        return jnp.einsum('bsd,ed->bse', out, w_o) + b_o

    def _L0_xattn_ref(k, v, q, ssm_kernel, D, head_dim):
        import jax, jax.numpy as jnp
        import numpy as np
        B, HD, L = k.shape
        H = HD // head_dim
        fft_size = 2 * L
        k_ = k.reshape(B, H, head_dim, L)
        v_ = v.reshape(B, H, head_dim, L)
        q_ = q.reshape(B, H, head_dim, L)
        kv = jnp.einsum('bhil,bhjl->bijhl', k_, v_)
        kv_f = jnp.fft.rfft(kv, n=fft_size)
        kernel_f = jnp.fft.rfft(ssm_kernel, n=fft_size)
        y = jnp.fft.irfft(kv_f * kernel_f, n=fft_size)[..., :L]
        out = y + kv * D[None, None, None, :, None]
        out = jnp.einsum('bijhl,bhil->bjhl', out, q_)
        out = jnp.transpose(out, (0, 2, 1, 3)).reshape(B, H * head_dim, L)
        return out.astype(k.dtype)

    def _L0_ffn_ref(hidden_states, router_w, w1, v1, w2, shared_gate, shared_up, shared_down):
        import jax, jax.numpy as jnp
        import numpy as np

        def _glu(x, wg, wu, wd):
            return jax.nn.silu(x @ wg) * (x @ wu) @ wd
        B, S, H = hidden_states.shape
        E = router_w.shape[0]
        TOP_K = 1
        x = hidden_states.reshape(-1, H)
        T = x.shape[0]
        logits = x @ router_w.T
        top_vals, top_idx = jax.lax.top_k(logits, TOP_K)
        expert_weights = jax.nn.sigmoid(top_vals)
        dense_w = jnp.zeros((T, E), x.dtype).at[jnp.arange(T)[:, None], top_idx].set(expert_weights)
        out = jnp.zeros_like(x)
        for e in range(E):
            y = _glu(x, w1[e], v1[e], w2[e])
            out = out + dense_w[:, e:e + 1] * y
        out = out + _glu(x, shared_gate.T, shared_up.T, shared_down.T)
        return out.reshape(B, S, H)

    def _L1_attn_ref(hidden_states, Wq, bq, Wk, bk, Wv, bv):
        import jax, jax.numpy as jnp
        import numpy as np
        import math
        HIDDEN = 256
        NUM_HEADS = 16
        HEAD_DIM = HIDDEN // NUM_HEADS
        BATCH = 2
        SEQ = 512
        BLOCK = 128
        TOPK = 64
        NEG = -1000000000.0

        def _split_heads(x):
            n, t, _ = x.shape
            return x.reshape(n, t, NUM_HEADS, HEAD_DIM).transpose(0, 2, 1, 3)

        def _local_attention(q, k, v):
            n, h, t, d = q.shape
            nb = t // BLOCK
            half = BLOCK // 2
            qb = q.reshape(n, h, nb, BLOCK, d)
            win = jnp.arange(nb)[:, None] * BLOCK - half + jnp.arange(2 * BLOCK)[None, :]
            valid = (win >= 0) & (win < t)
            winc = jnp.clip(win, 0, t - 1)
            kb = k[:, :, winc, :]
            vb = v[:, :, winc, :]
            scores = jnp.einsum('nhbqd,nhbkd->nhbqk', qb, kb) / math.sqrt(d)
            scores = jnp.where(valid[None, None, :, None, :], scores, NEG)
            probs = jax.nn.softmax(scores, axis=-1)
            ctx = jnp.einsum('nhbqk,nhbkd->nhbqd', probs, vb)
            return ctx.reshape(n, h, t, d)

        def _global_index(q):
            n, h, t, d = q.shape
            norm = jnp.linalg.norm(q, axis=-1)
            _, top_idx = jax.lax.top_k(norm, TOPK - 2)
            bos = jnp.zeros((n, h, 1), jnp.int32)
            eos = jnp.full((n, h, 1), t - 1, jnp.int32)
            return jnp.concatenate([bos, top_idx.astype(jnp.int32), eos], axis=-1)
        q = _split_heads(hidden_states @ Wq + bq)
        k = _split_heads(hidden_states @ Wk + bk)
        v = _split_heads(hidden_states @ Wv + bv)
        n, h, t, d = q.shape
        ctx = _local_attention(q, k, v)
        idx = _global_index(q)
        qg = jnp.take_along_axis(q, idx[..., None], axis=-2)
        g_scores = jnp.einsum('nhqd,nhkd->nhqk', qg, k) / math.sqrt(d)
        g_probs = jax.nn.softmax(g_scores, axis=-1)
        g_ctx = jnp.einsum('nhqk,nhkd->nhqd', g_probs, v)
        bn = jnp.arange(n)[:, None, None]
        bh = jnp.arange(h)[None, :, None]
        ctx = ctx.at[bn, bh, idx].set(g_ctx)
        out = ctx.transpose(0, 2, 1, 3).reshape(n, t, h * d)
        return out

    def _L1_xattn_ref(hidden_states, memory_tokens, memory_mask):
        import jax, jax.numpy as jnp
        import numpy as np
        B, S, D = hidden_states.shape
        scale = 1.0 / jnp.sqrt(jnp.asarray(D, hidden_states.dtype))
        scores = jnp.einsum('bsd,bmd->bsm', hidden_states, memory_tokens) * scale
        neg_inf = jnp.asarray(-1e+30, scores.dtype)
        scores = jnp.where(memory_mask[:, None, :], scores, neg_inf)
        attn = jax.nn.softmax(scores, axis=-1)
        readout = jnp.einsum('bsm,bmd->bsd', attn, memory_tokens)
        valid_b = jnp.any(memory_mask, axis=-1)
        out = jnp.where(valid_b[:, None, None], readout, jnp.zeros_like(readout))
        return out

    def _L1_ffn_ref(x, w1, b1, ln_g, ln_b, w2, b2):
        import jax, jax.numpy as jnp
        import numpy as np
        EPS = 1e-05

        def rms_norm(x):
            return x * jax.lax.rsqrt(jnp.mean(x * x, axis=-1, keepdims=True) + EPS)

        def act_quant(x):
            scale = 127.0 / jnp.clip(jnp.max(jnp.abs(x), axis=-1, keepdims=True), 1e-05)
            q = jnp.clip(jnp.round(x * scale), -128.0, 127.0) / scale
            return x + jax.lax.stop_gradient(q - x)

        def weight_quant(w):
            scale = 1.0 / jnp.clip(jnp.mean(jnp.abs(w)), 1e-05)
            q = jnp.clip(jnp.round(w * scale), -1.0, 1.0) / scale
            return w + jax.lax.stop_gradient(q - w)

        def bitlinear158(x, w, b):
            xq = act_quant(rms_norm(x))
            wq = weight_quant(w)
            return jnp.einsum('bsd,od->bso', xq, wq) + b

        def layer_norm(x, g, b):
            mu = jnp.mean(x, axis=-1, keepdims=True)
            var = jnp.mean((x - mu) ** 2, axis=-1, keepdims=True)
            return (x - mu) * jax.lax.rsqrt(var + EPS) * g + b
        h = jax.nn.silu(bitlinear158(x, w1, b1))
        h = jax.nn.gelu(h, approximate=False)
        h = layer_norm(h, ln_g, ln_b)
        return bitlinear158(h, w2, b2)
    x = x + _L0_attn_ref(_layernorm(x, axis=-1), L0_attn_w_qkv, L0_attn_b_qkv, L0_attn_w_o, L0_attn_b_o)
    x = x + _L0_xattn_ref(ctx_2048, ctx_2048, _layernorm(x, axis=-1), L0_xattn_ssm_kernel, L0_xattn_D, 8)
    x = x + _L0_ffn_ref(_layernorm(x, axis=-1), L0_ffn_router_w, L0_ffn_w1, L0_ffn_v1, L0_ffn_w2, L0_ffn_shared_gate, L0_ffn_shared_up, L0_ffn_shared_down)
    x = x + _L1_attn_ref(_layernorm(x, axis=-1), L1_attn_Wq, L1_attn_bq, L1_attn_Wk, L1_attn_bk, L1_attn_Wv, L1_attn_bv)
    x = x + _L1_xattn_ref(_layernorm(x, axis=-1), ctx_2048, mask_BxS2_bk0)
    x = x + _L1_ffn_ref(_layernorm(x, axis=-1), L1_ffn_w1, L1_ffn_b1, L1_ffn_ln_g, L1_ffn_ln_b, L1_ffn_w2, L1_ffn_b2)
    return x

_drawn_inputs = setup_inputs


def setup_inputs(seed=0):
    import zlib

    import numpy as np

    out = dict(_drawn_inputs(seed))
    spreads = {'L0_attn_b_qkv': (0.0, 0.1),
     'L0_attn_b_o': (0.0, 0.1),
     'L1_attn_bq': (0.0, 0.8),
     'L1_attn_bk': (0.0, 2.0),
     'L1_attn_bv': (0.0, 2.0),
     'L1_ffn_b1': (0.0, 2.0),
     'L1_ffn_ln_g': (1.0, 0.6),
     'L1_ffn_ln_b': (0.0, 2.0),
     'L1_ffn_b2': (0.0, 2.0)}
    factors = {'L0_ffn_router_w': 8.0,
     'L0_ffn_w1': 8.0,
     'L0_ffn_v1': 8.0,
     'L0_ffn_w2': 8.0,
     'L0_ffn_shared_gate': 8.0,
     'L0_ffn_shared_up': 8.0,
     'L0_ffn_shared_down': 8.0,
     'L1_attn_Wq': 8.0,
     'L1_attn_Wk': 8.0,
     'L1_attn_Wv': 8.0,
     'L1_ffn_w1': 5.646,
     'L1_ffn_w2': 5.111}
    for name, (base, spread) in spreads.items():
        noise = np.random.default_rng([zlib.crc32(name.encode()), seed]).standard_normal(out[name].shape)
        drawn = base * np.exp(spread * noise) if base else spread * noise
        out[name] = jnp.asarray(drawn.astype(out[name].dtype))
    for name, factor in factors.items():
        out[name] = (out[name] * factor).astype(out[name].dtype)
    return out
```

```python
from contextlib import ExitStack

import concourse.bass as bass
from concourse import mybir
from concourse.bass import ds

P = 128
NB = 16
D = 256
KT = D // P
NH = 16
HD = D // NH
GR = 4
GH = NH // GR
VW = 32
NE = 8
NI = 256
NS = 24
CH = 16
CD = P // CH
INNER = 1024
EPS = 1e-5
NEG = 1e30
MAGIC = 12582912.0
ATT_SCALE = float(HD) ** -0.5

F32 = mybir.dt.float32
BF16 = mybir.dt.bfloat16
U32 = mybir.dt.uint32
I32 = mybir.dt.int32
U8 = mybir.dt.uint8
ALU = mybir.AluOpType
ACT = mybir.ActivationFunctionType
AX = mybir.AxisListType


def wait(eng, sem, value):
    if isinstance(value, int) and value <= 0:
        return
    eng.wait_ge(sem, value)


def there(t):
    return not isinstance(t, int) or 0 <= t < NB


def pipeline(eng, body, ahead=1, behind=2, first=4):
    last = (NB - ahead) - (NB - ahead) % 2
    for t in range(first):
        body(t, t % 2, t // 2)
    with eng.Fori(first // 2, last // 2) as i:
        for u in range(2):
            body(2 * i + u, u, i)
    for t in range(last, NB + behind):
        body(t, t % 2, t // 2)


class Stage:
    def __init__(self, tensor, scalar, vector, gpsimd, x_ready=None, sync=None, summed=None,
                 scattered=None, zeroed=None, pool_zero=None):
        self.tensor, self.scalar, self.vector, self.gpsimd = tensor, scalar, vector, gpsimd
        self.x_ready, self.sync, self.summed = x_ready, sync, summed
        self.scattered, self.zeroed, self.pool_zero = scattered, zeroed, pool_zero


def build(nc, a, out, stages=6):
    ctx = ExitStack()
    with ctx:
        def sb(name, cols, dt=F32, rows=P):
            return ctx.enter_context(nc.sbuf_tensor(name, [rows, cols], dt))[:, :]

        def sem(name):
            return ctx.enter_context(nc.semaphore(name))

        x = sb("x", NB * D)
        xnT_all = sb("xnT_all", KT * NB * P)
        xn_all = sb("xn_all", NB * D)
        wide = sb("wide", NB * INNER)
        w_ex = wide[:, 0:KT * NE * 3 * NI]
        outT = wide[:, KT * NE * 3 * NI:]
        ctx_sb = sb("ctx_sb", NB * D)
        ctxT = sb("ctxT", KT * NB * P)
        w_qkv = [sb(f"w_qkv{n}", KT * 3 * D) for n in range(2)]
        w_o = sb("w_o", KT * D)
        w_sh = sb("w_sh", KT * 3 * D)
        WORK = 6144
        work = sb("work", WORK)
        bn = sb("bn", 2 * 6 * 2)
        mv = sb("mv", 2 * 2)
        var_eps = sb("var_eps", 2)
        rstd = sb("rstd", 2)
        xn = sb("xn", 2 * D)
        xnT = sb("xnT", 2 * D)
        qk_cols = sb("qk_cols", 2 * 6)
        of_head = sb("of_head", GH)
        powers = sb("powers", 4)
        tick = sb("tick", 1)
        ident = sb("ident", P)
        row_bias = sb("row_bias", 3 * D)
        rw = sb("rw", KT * NE)
        SMALL = 2048
        small = sb("small", SMALL)
        ident_bf = sb("ident_bf", P, BF16)
        tri = sb("tri", P)
        tri_bf = sb("tri_bf", P, BF16)
        ones_bf = sb("ones_bf", P, BF16)
        slot_iota = sb("slot_iota", NS + NE + NE * NE)
        ps = [ctx.enter_context(nc.psum_tensor(f"ps{k}", [P, 512], F32))[:, :] for k in range(8)]

        kt_x = lambda ap, n: ap.rearrange("p (c n) -> p c n", n=n)
        xnT_all3 = kt_x(xnT_all, NB * P)
        outT3 = kt_x(outT, NB * P)
        ctxT3 = kt_x(ctxT, NB * P)
        ctxR3 = kt_x(xn_all, NB * P)
        w_qkv3 = [kt_x(w, 3 * D) for w in w_qkv]
        w_o3 = kt_x(w_o, D)
        w_sh_gu = kt_x(w_sh[:, 0:KT * 2 * D], 2 * D)
        w_sh_d = kt_x(w_sh[:, KT * 2 * D:], D)
        w_ex_gu = kt_x(w_ex[:, 0:KT * NE * 2 * NI], NE * 2 * NI)
        w_ex_d = kt_x(w_ex[:, KT * NE * 2 * NI:], NE * D)
        rw3 = kt_x(rw, NE)
        slot2 = lambda ap, u, n: ap[:, u * n:(u + 1) * n]
        tile_of = lambda ap, t, n=D: ap[:, ds(t * n, n)]

        hank = nc.dram_tensor("hank", [CH, 2 * D], F32).ap()
        sorted_x = nc.dram_tensor("sorted_x", [NS * P, D], F32).ap()
        sorted_y = nc.dram_tensor("sorted_y", [NS * P, D], F32).ap()

        x_loaded0, x_loaded1 = sem("x_loaded0"), sem("x_loaded1")
        attn_loaded = [sem("attn0_loaded"), sem("attn1_loaded")]
        const_loaded = sem("const_loaded")
        conv_loaded = sem("conv_loaded")
        ctx_loaded = sem("ctx_loaded")
        moe_loaded = sem("moe_loaded")
        zero_stored = sem("zero_stored")
        out_stored = sem("out_stored")
        bf_ready = sem("bf_ready")

        FIRST = 3
        block = ctx.enter_context(nc.Block())

        front_sem = {k: sem("front_" + k) for k in (
            "bn_done", "stats", "eps_done", "rstd", "xn", "xnT_ps", "xnT")}

        class Front:
            def __init__(self, stage, x_ready, own_x=False):
                self.base = NB * stage
                self.turned = True
                self.own_x = own_x
                self.x_ready = x_ready
                self.bn_done, self.stats = front_sem["bn_done"], front_sem["stats"]
                self.eps_done, self.rstd = front_sem["eps_done"], front_sem["rstd"]
                self.xn, self.xnT_ps = front_sem["xn"], front_sem["xnT_ps"]
                self.xnT = front_sem["xnT"]

        def front_stats(dve, f, t, u):
            f.x_ready(dve, t)
            if f.own_x:
                dve.memset(tick, 0.0)
            dve.bn_stats(slot2(bn, u, 6), tile_of(x, t)).then_inc(f.bn_done, 1)
            dve.wait_ge(f.bn_done, f.base + t + 1)
            dve.memset(tick, 0.0)
            dve.bn_aggr(slot2(mv, u, 2), slot2(bn, u, 6)).then_inc(f.stats, 1)

        def front_rstd(pool, f, t, u):
            pool.wait_ge(f.stats, f.base + t + 1)
            pool.tensor_tensor(var_eps[:, u:u + 1], mv[:, 2 * u + 1:2 * u + 2], powers[:, 1:2],
                               ALU.add).then_inc(f.eps_done, 1)
            pool.wait_ge(f.eps_done, f.base + t + 1)
            pool.tensor_tensor(rstd[:, u:u + 1], var_eps[:, u:u + 1], powers[:, 0:1],
                               ALU.pow).then_inc(f.rstd, 1)

        def front_xn(dve, f, t, u, readers=()):
            dve.wait_ge(f.rstd, f.base + t + 1)
            if f.turned:
                wait(dve, f.xnT_ps, f.base + t - 1)
            for s, v in readers:
                wait(dve, s, v)
            dve.tensor_scalar(slot2(xn, u, D), tile_of(x, t), mv[:, 2 * u:2 * u + 1],
                              rstd[:, u:u + 1], ALU.subtract, ALU.mult).then_inc(f.xn, 1)

        def front_transpose(pe, f, t, u, bank):
            pe.wait_ge(f.xn, f.base + t + 1)
            wait(pe, f.xnT, f.base + t)
            for c in range(KT):
                mm = pe.transpose(bank[:, c * P:(c + 1) * P], xn[:, u * D + c * P:u * D + (c + 1) * P],
                                  ident)
            mm.then_inc(f.xnT_ps, 1)

        def front_copy(act, f, t, u, bank, free, freed):
            act.wait_ge(f.xnT_ps, f.base + t + 1)
            wait(act, free, freed)
            act.copy(slot2(xnT, u, D), bank[:, 0:D]).then_inc(f.xnT, 1)

        att_sem = {k: sem("att_" + k) for k in (
            "qv_ps", "k_ps", "q_sb", "k_sb", "v_sb", "s_ps", "mx", "sub", "exp", "pT_ps", "pT",
            "pv", "oT", "ot_ps", "rsum", "att", "attT_ps", "attT", "o_ps", "x_bias", "x_new", "ones")}

        def attention(layer, x_ready, before):
            f = Front(3 * layer, x_ready)
            s = att_sem
            B = NB * layer
            o = 0
            prob = [work[:, r * 512:(r + 1) * 512] for r in range(GR)]
            o += GR * 512
            qT = [kt_x(work[:, o + u * D:o + (u + 1) * D], P) for u in range(2)]
            o += 2 * D
            va = [work[:, o + u * NH * VW:o + (u + 1) * NH * VW].rearrange("p (h w) -> p h w", w=VW)
                  for u in range(2)]
            o += 2 * NH * VW
            att = work[:, o:o + D]
            o += D
            attT = kt_x(work[:, o:o + D], P)
            o += D
            oT = work[:, o:o + 512]
            o += 512
            mxs = work[:, o:o + 4 * GR]
            rsum = work[:, o + 16:o + 32]
            assert o + 32 <= WORK
            kTm = [kt_x(outT[:, u * 1024:(u + 1) * 1024], 512) for u in range(2)]
            probT = [outT[:, 2048 + r * 512:2048 + (r + 1) * 512] for r in range(2)]
            S, T, O, X, QV, KO = ps[0:2], ps[2:4], ps[4], ps[5], ps[6], ps[7]
            O3 = O.rearrange("p (h w) -> p h w", w=VW)
            bias = qk_cols[:, 6 * layer:6 * layer + 6]
            w = w_qkv3[layer]

            def pe_scores(pe, t, u, r):
                wait(pe, s["sub"], 4 * B + 4 * t + r - 1)
                c, rows = r // 2, slice(64 * (r % 2), 64 * (r % 2) + 64)
                pe.matmul(S[r % 2], qT[u][rows, c, :], kTm[u][rows, c, :], start=True, stop=True
                          ).then_inc(s["s_ps"], 1)

            def pe_turn(pe, t, u, r):
                pe.wait_ge(s["exp"], 4 * B + 4 * t + r + 1)
                wait(pe, s["pT"], 4 * B + 4 * t + r - 1)
                for h in range(GH):
                    mm = pe.transpose(T[r % 2][:, h * P:(h + 1) * P], prob[r][:, h * P:(h + 1) * P],
                                      ident)
                mm.then_inc(s["pT_ps"], 1)

            def pe_pv(pe, t, u, r):
                pe.wait_ge(s["pT"], 4 * B + 4 * t + r + 1)
                if r == 0:
                    pe.wait_ge(s["v_sb"], B + t + 1)
                    wait(pe, s["att"], B + t)
                for k in range(GH):
                    mm = pe.matmul(O[VW * k:VW * k + VW, r * P:(r + 1) * P], va[u][:, GH * r + k, :],
                                   probT[r % 2][:, k * P:(k + 1) * P], start=True, stop=True,
                                   skip_group_check=True)
                mm.then_inc(s["pv"], 1)

            def pe_o_turn(pe, t):
                pe.wait_ge(s["oT"], B + t + 1)
                for r in range(GR):
                    mm = pe.transpose(O[:, r * P:(r + 1) * P], oT[:, r * P:(r + 1) * P], ident)
                mm.then_inc(s["ot_ps"], 1)

            def pe_qkv(pe, t, u):
                xT = lambda c: xnT[:, u * D + c * P:u * D + (c + 1) * P]
                pe.wait_ge(f.xnT, f.base + t + 1)
                wait(pe, s["q_sb"], 2 * B + 2 * t)
                wait(pe, s["v_sb"], B + t)
                for j in range(2):
                    for c in range(KT):
                        pe.matmul(QV[:, j * P:(j + 1) * P], w[:, c, j * P:(j + 1) * P], xT(c),
                                  start=(c == 0), stop=(c == KT - 1), skip_group_check=True)
                for c in range(KT):
                    mm = pe.matmul(QV[:, D:2 * D], xT(c), w[:, c, 2 * D:3 * D], start=(c == 0),
                                   stop=(c == KT - 1), skip_group_check=True)
                mm.then_inc(s["qv_ps"], 1)
                wait(pe, s["k_sb"], 2 * B + 2 * t)
                if layer == 0:
                    wait(pe, s["x_new"], B + t - 2)
                for j in range(2):
                    for c in range(KT):
                        mm = pe.matmul(KO[:, j * P:(j + 1) * P], w[:, c, D + j * P:D + (j + 1) * P],
                                       xT(c), start=(c == 0), stop=(c == KT - 1),
                                       skip_group_check=True)
                mm.then_inc(s["k_ps"], 1)

            def pe_att_turn(pe, t, xnT_before):
                pe.wait_ge(s["att"], B + t + 1)
                wait(pe, s["attT"], 2 * t)
                wait(pe, f.xnT, f.base + xnT_before)
                for c in range(KT):
                    mm = pe.transpose(X[:, D + c * P:D + (c + 1) * P], att[:, c * P:(c + 1) * P], ident)
                mm.then_inc(s["attT_ps"], 1)

            def pe_out(pe, t):
                pe.wait_ge(s["attT"], 2 * (t + 1))
                wait(pe, s["x_new"], B + t)
                for c in range(KT):
                    mm = pe.matmul(KO[:, D:2 * D], attT[:, c, :], w_o3[:, c, :], start=(c == 0),
                                   stop=(c == KT - 1), skip_group_check=True)
                mm.then_inc(s["o_ps"], 1)

            def pe_body(pe, t, u, i):
                for r in range(GR):
                    if there(t):
                        if r == 0:
                            pe.wait_ge(s["q_sb"], 2 * B + 2 * (t + 1))
                            pe.wait_ge(s["k_sb"], 2 * B + 2 * (t + 1))
                        pe_scores(pe, t, u, r)
                    if r < 2 and there(t - 1):
                        pe_turn(pe, t - 1, 1 - u, r + 2)
                        pe_pv(pe, t - 1, 1 - u, r + 1)
                    if r == 1 and layer == 0 and there(t - 2):
                        pe_out(pe, t - 2)
                    if r == 1 and there(t + 1):
                        if layer == 0:
                            wait(pe, s["attT"], 2 * (t - 1))
                        front_transpose(pe, f, t + 1, 1 - u, X)
                    if r >= 2 and there(t):
                        pe_turn(pe, t, u, r - 2)
                    if r == 2:
                        if there(t - 1):
                            pe_pv(pe, t - 1, 1 - u, 3)
                        if there(t + 1):
                            pe_qkv(pe, t + 1, 1 - u)
                        if there(t - 1):
                            pe_o_turn(pe, t - 1)
                    if r == 3:
                        if there(t):
                            pe_pv(pe, t, u, 0)
                        if layer == 0 and there(t - 1):
                            pe_att_turn(pe, t - 1, min(t + 2, NB) if isinstance(t, int) else t + 2)

            def tensor(pe):
                pe.wait_ge(const_loaded, 16 * N_CONST)
                pe.wait_ge(attn_loaded[layer], 16 * N_ATTN[layer])
                before(pe)
                front_transpose(pe, f, 0, 0, X)
                pe_qkv(pe, 0, 0)
                pipeline(pe, lambda t, u, i: pe_body(pe, t, u, i))

            def act_exp(act, t, r):
                act.wait_ge(s["sub"], 4 * B + 4 * t + r + 1)
                act.activation(prob[r], prob[r], ACT.Exp, scale=ATT_SCALE).then_inc(s["exp"], 1)

            def act_copy(act, t, r):
                act.wait_ge(s["pT_ps"], 4 * B + 4 * t + r + 1)
                wait(act, s["pv"], 4 * B + 4 * t + r - 1)
                act.copy(probT[r % 2], T[r % 2]).then_inc(s["pT"], 1)

            def act_qv(act, t, u):
                act.wait_ge(s["qv_ps"], B + t + 1)
                wait(act, s["s_ps"], 4 * B + 4 * (t - 1))
                for c in range(KT):
                    act.activation(qT[u][:, c, :], QV[:, c * P:(c + 1) * P], ACT.Identity,
                                   bias=bias[:, c:c + 1]).then_inc(s["q_sb"], 1)
                wait(act, s["pv"], 4 * B + 4 * (t - 1))
                act.copy(va[u][:, :, 0:HD], QV[:, D:2 * D].rearrange("p (h w) -> p h w", w=HD)
                         ).then_inc(s["v_sb"], 1)

            def act_oT(act, t):
                act.wait_ge(s["pv"], 4 * B + 4 * (t + 1))
                wait(act, s["ot_ps"], B + t)
                act.copy(oT, O).then_inc(s["oT"], 1)

            def act_attT(act, t):
                act.wait_ge(s["attT_ps"], t + 1)
                wait(act, s["o_ps"], t)
                for c in range(KT):
                    act.activation(attT[:, c, :], X[:, D + c * P:D + (c + 1) * P], ACT.Identity,
                                   bias=bias[:, 4 + c:5 + c]).then_inc(s["attT"], 1)

            def act_body(act, t, u, i):
                for r in range(GR):
                    if there(t):
                        act_exp(act, t, r)
                    if r < 2 and there(t - 1):
                        act_copy(act, t - 1, r + 2)
                    if r >= 2 and there(t):
                        act_copy(act, t, r - 2)
                    if r == 1 and there(t + 1):
                        front_copy(act, f, t + 1, 1 - u, X, s["k_ps"], B + t)
                    if r == 2 and there(t - 1):
                        act_oT(act, t - 1)
                    if r == 2 and there(t + 1):
                        act_qv(act, t + 1, 1 - u)
                    if r == 3 and layer == 0 and there(t - 1):
                        act_attT(act, t - 1)

            def scalar(act):
                act.wait_ge(const_loaded, 16 * N_CONST)
                before(act)
                act.wait_ge(s["ones"], 2 * layer + 2)
                front_copy(act, f, 0, 0, X, s["k_ps"], B)
                act_qv(act, 0, 0)
                pipeline(act, lambda t, u, i: act_body(act, t, u, i), first=2)

            def dve_softmax(dve, t, r):
                bank = S[r % 2].rearrange("p (h k) -> p h k", k=P)
                m = mxs[:, 4 * r:4 * r + 4]
                dve.wait_ge(s["s_ps"], 4 * B + 4 * t + r + 1)
                dve.tensor_reduce(m, bank, AX.X, ALU.max).then_inc(s["mx"], 1)
                dve.wait_ge(s["mx"], 4 * B + 4 * t + r + 1)
                wait(dve, s["pT_ps"], 4 * B + 4 * (t - 1) + r + 1)
                dve.tensor_tensor(prob[r].rearrange("p (h k) -> p h k", k=P), bank,
                                  m.unsqueeze(2).broadcast_to([P, GH, P]),
                                  ALU.subtract).then_inc(s["sub"], 1)

            def dve_keys(dve, t, u):
                dve.wait_ge(s["k_ps"], B + t + 1)
                wait(dve, s["s_ps"], 4 * B + 4 * (t - 1))
                for c in range(KT):
                    dve.scalar_tensor_tensor(
                        kTm[u][:, c, :].rearrange("p (e k) -> p e k", k=P),
                        KO[:, c * P:(c + 1) * P].unsqueeze(1).broadcast_to([P, GH, P]),
                        bias[:, 2 + c:3 + c], of_head.unsqueeze(2).broadcast_to([P, GH, P]),
                        ALU.add, ALU.mult).then_inc(s["k_sb"], 1)

            def dve_att(dve, t):
                dve.wait_ge(s["ot_ps"], B + t + 1)
                dve.reciprocal(rsum, O3[:, :, HD]).then_inc(s["rsum"], 1)
                dve.wait_ge(s["rsum"], B + t + 1)
                if layer == 0:
                    wait(dve, s["attT_ps"], t)
                else:
                    wait(dve, s["x_new"], B + t)
                dve.tensor_tensor(att.rearrange("p (h w) -> p h w", w=HD), O3[:, :, 0:HD],
                                  rsum.unsqueeze(2).broadcast_to([P, NH, HD]),
                                  ALU.mult).then_inc(s["att"], 1)

            def dve_x(dve, t):
                dve.wait_ge(s["x_bias"], B + t + 1)
                if layer == 0:
                    dve.wait_ge(s["o_ps"], t + 1)
                    add = KO[:, D:2 * D]
                else:
                    dve.wait_ge(s["att"], B + t + 1)
                    add = att
                dve.tensor_tensor(tile_of(x, t), tile_of(x, t), add, ALU.add).then_inc(s["x_new"], 1)

            def dve_body(dve, t, u, i):
                if there(t + 1):
                    front_stats(dve, f, t + 1, 1 - u)
                for r in range(GR):
                    if there(t):
                        dve_softmax(dve, t, r)
                    if r == 0 and there(t + 1):
                        front_xn(dve, f, t + 1, 1 - u)
                    if r == 1 and layer == 0 and there(t - 2):
                        dve_x(dve, t - 2)
                    if r == 2 and there(t - 1):
                        dve_att(dve, t - 1)
                    if r == 3 and layer == 1 and there(t - 1):
                        dve_x(dve, t - 1)
                    if r == 3 and there(t + 1):
                        dve_keys(dve, t + 1, 1 - u)

            def vector(dve):
                dve.wait_ge(const_loaded, 16 * N_CONST)
                before(dve)
                for u in range(2):
                    dve.memset(va[u], 1.0).then_inc(s["ones"], 1)
                front_stats(dve, f, 0, 0)
                front_xn(dve, f, 0, 0)
                dve_keys(dve, 0, 0)
                pipeline(dve, lambda t, u, i: dve_body(dve, t, u, i), first=2)

            def pool_body(pool, t, u, i):
                if there(t + 1):
                    front_rstd(pool, f, t + 1, 1 - u)
                if there(t):
                    pool.wait_ge(f.xn, f.base + t + 1)
                    pool.tensor_tensor(tile_of(x, t), tile_of(x, t),
                                       row_bias[:, layer * D:(layer + 1) * D],
                                       ALU.add).then_inc(s["x_bias"], 1)

            def gpsimd(pool):
                pool.wait_ge(const_loaded, 16 * N_CONST)
                front_rstd(pool, f, 0, 0)
                pipeline(pool, lambda t, u, i: pool_body(pool, t, u, i), first=2)

            return Stage(tensor=tensor, scalar=scalar, vector=vector, gpsimd=gpsimd,
                                   x_ready=lambda eng, t: wait(eng, s["x_new"], B + t + 1))

        def convolution(x_ready, before):
            f = Front(1, x_ready)
            s = {k: sem(f"conv_{k}") for k in (
                "toep0", "toep1", "kv", "conv", "prod", "sum")}
            kv = [kt_x(work[:, u * 2048:(u + 1) * 2048], 1024) for u in range(2)]
            toep = [kt_x(work[:, 4096 + u * 512:4096 + (u + 1) * 512], D) for u in range(2)]
            prod = [work[:, 5120 + u * 512:5120 + (u + 1) * 512] for u in range(2)]
            X = ps[4:6]

            def body_c1(eng, name):
                def dve(t, u, i):
                    if there(t):
                        front_stats(eng, f, t, u)
                    if there(t - 1):
                        front_xn(eng, f, t - 1, 1 - u)
                def pool(t, u, i):
                    if there(t):
                        front_rstd(eng, f, t, u)
                def pe(t, u, i):
                    if there(t):
                        front_transpose(eng, f, t, u, X[0])
                def act(t, u, i):
                    if there(t):
                        eng.wait_ge(f.xnT_ps, f.base + t + 1)
                        eng.copy(xnT_all3[:, :, ds(t * P, P)], kt_x(X[0][:, 0:D], P)
                                 ).then_inc(f.xnT, 1)
                return {"dve": dve, "pool": pool, "pe": pe, "act": act}[name]

            def load_toep(sp, h, u, i):
                row = hank[ds(h, 1), :]
                for c in range(KT):
                    src = bass.AP(row.tensor, row.offset + c * P, [[1, P], [1, D]])
                    sp.dma_start(toep[u][:, c, :], src).then_inc(s[f"toep{u}"], 16)

            def sync(sp):
                before(sp)
                sp.wait_ge(hank_stored, 16)
                for h in range(2):
                    load_toep(sp, h, h, 0)
                with sp.Fori(1, CH // 2) as i:
                    for u in range(2):
                        h = 2 * i + u
                        sp.wait_ge(s["conv"], 4 * (h - 1))
                        load_toep(sp, h, u, i)

            def tensor(pe):
                before(pe)
                pipeline(pe, body_c1(pe, "pe"), 0, 0)
                with pe.Fori(0, CH // 2) as i:
                    for u in range(2):
                        h = 2 * i + u
                        pe.wait_ge(s[f"toep{u}"], 32 * (i + 1))
                        pe.wait_ge(s["kv"], 2 * (h + 1))
                        for o in range(4):
                            lt, half = o // 2, o % 2
                            pe.wait_ge(s["prod"], 4 * h + o + 1)
                            for c in range(1 - lt, KT):
                                mm = pe.matmul(ps[4 * u + o], toep[u][:, c, lt * P:(lt + 1) * P],
                                               kv[u][:, c, half * 512:(half + 1) * 512],
                                               start=(c == 1 - lt), stop=(c == KT - 1))
                            mm.then_inc(s["conv"], 1)

            def scalar(act):
                pipeline(act, body_c1(act, "act"), 0, 0)

            def pool_kv(pool, h, u, guard):
                src = ctxR3.rearrange("p c (b n) -> p c b n", n=P)
                for c in range(KT):
                    chan = src[:, c, :, ds(h * CD, CD)]
                    pool.tensor_tensor(
                        kv[u][:, c, :].rearrange("p (b i j) -> p b i j", i=CD, j=CD),
                        chan.unsqueeze(3).broadcast_to([P, NB, CD, CD]),
                        chan.unsqueeze(2).broadcast_to([P, NB, CD, CD]),
                        ALU.mult).then_inc(s["kv"], 1)

            def gpsimd(pool):
                pipeline(pool, body_c1(pool, "pool"), 0, 0)
                before(pool)
                pool.wait_ge(conv_loaded, 16)
                for h in range(2):
                    pool_kv(pool, h, h, None)
                with pool.Fori(1, CH // 2) as i:
                    for u in range(2):
                        h = 2 * i + u
                        pool.wait_ge(s["conv"], 4 * (h - 1))
                        pool_kv(pool, h, u, None)

            def dve_prod(dve, h, u, o):
                lt, half = o // 2, o % 2
                q = xnT_all3[:, lt, half * 1024:(half + 1) * 1024].rearrange("p (b n) -> p b n", n=P)
                dve.wait_ge(s["sum"], 4 * h + o + 1)
                dve.wait_ge(s["conv"], 4 * h + o + 1)
                dve.tensor_tensor(prod[o % 2].rearrange("p (b i j) -> p b i j", i=CD, j=CD),
                                  ps[4 * u + o].rearrange("p (b i j) -> p b i j", i=CD, j=CD),
                                  q[:, :, ds(h * CD, CD)].unsqueeze(3).broadcast_to([P, NB // 2, CD, CD]),
                                  ALU.mult).then_inc(s["prod"], 1)

            def dve_sum(dve, h, o):
                lt, half = o // 2, o % 2
                dst = outT3[:, lt, half * 1024:(half + 1) * 1024].rearrange("p (b n) -> p b n", n=P)
                dve.wait_ge(s["prod"], 8 + 4 * h + o + 1)
                dve.tensor_reduce(dst[:, :, ds(h * CD, CD)],
                                  prod[o % 2].rearrange("p (b i j) -> p b j i", i=CD, j=CD),
                                  AX.X, ALU.add).then_inc(s["sum"], 1)

            def vector(dve):
                pipeline(dve, body_c1(dve, "dve"), 0, 1)
                dve.wait_ge(f.xnT, f.base + NB)
                dve.engine_nop().then_inc(s["prod"], 8)
                dve.engine_nop().then_inc(s["sum"], 2)
                with dve.Fori(0, CH // 2) as i:
                    for u in range(2):
                        h = 2 * i + u
                        dve_prod(dve, h, u, 0)
                        for o in range(4):
                            if o < 3:
                                dve_prod(dve, h, u, o + 1)
                            dve_sum(dve, h, o)

            return Stage(sync=sync, tensor=tensor, scalar=scalar, vector=vector,
                                   gpsimd=gpsimd, summed=s["sum"])

        def experts(conv_done):
            s = {k: sem(f"moe_{k}") for k in (
                "oT", "o_ps", "x_conv", "kept", "lg_ps", "lg", "route", "rank", "count", "zero",
                "gate_exp", "gate", "pos", "expert", "zeroed", "scattered", "sh_g0", "sh_g1",
                "sh_silu", "sh_u0", "sh_u1", "sh_h", "sh_y", "x_shared",
                "xs0", "xs1", "xsT_ps", "xsT", "gu", "silu", "h", "hT_ps", "hT", "y_ps", "y",
                "stored0", "stored1", "x_new")}
            gathered = [sem(f"moe_gathered{n}") for n in range(4)]
            f = Front(2, lambda eng, t: eng.wait_ge(s["x_conv"], t + 1), True)
            xs = [work[:, u * D:(u + 1) * D] for u in range(2)]
            oT = xs
            xsT = [work[:, 512 + u * D:512 + (u + 1) * D] for u in range(2)]
            silu = [work[:, 1024 + u * D:1024 + (u + 1) * D] for u in range(2)]
            h = [work[:, 1536 + u * D:1536 + (u + 1) * D] for u in range(2)]
            hT = [work[:, 2048 + u * D:2048 + (u + 1) * D] for u in range(2)]
            y = [work[:, 2560 + u * D:2560 + (u + 1) * D] for u in range(2)]
            sh_silu = [work[:, 3072 + c * 512:3072 + (c + 1) * 512] for c in range(2)]
            sh_h = [kt_x(work[:, 4096 + u * 1024:4096 + (u + 1) * 1024], 512) for u in range(2)]
            returned = xnT_all

            o = [800]
            def cut(n):
                o[0] += n
                assert o[0] <= SMALL
                return small[:, o[0] - n:o[0]]
            te = lambda ap: ap.rearrange("p (t e) -> p t e", e=NE)
            lg, eq, pr, val = cut(128), cut(128), cut(128), cut(128)
            onehot = cut(64).bitcast(BF16)
            mx, m2, gate_e, gate, posf = cut(16), cut(16), cut(16), cut(16), cut(16)
            pos = cut(16).bitcast(U32)
            slots_of, slot_prod, first_slot, first_row = cut(8), cut(64), cut(8), cut(8)
            cmp, esum = cut(NS * NE), cut(NS)
            expert_of = cut(NS).bitcast(I32)
            zeros = small[:, 520:776]
            slot_no, prefer, lower = slot_iota[:, 0:NS], slot_iota[:, NS:NS + NE], slot_iota[:, NS + NE:]
            RANK, COUNT = ps[4][:, 0:P], ps[5][:, 0:NE]

            def act_route(act, t, u, i):
                if there(t):
                    wait(act, s["o_ps"], t - 1)
                    act.copy(kt_x(oT[u], P), outT3[:, :, ds(t * P, P)]).then_inc(s["oT"], 1)
                if there(t - 2):
                    act.wait_ge(f.xnT_ps, f.base + t - 1)
                    wait(act, s["lg_ps"], t - 3)
                    wait(act, s["kept"], 2 * (t - 3))
                    act.copy(slot2(xnT, u, D), ps[2][:, 0:D]).then_inc(f.xnT, 1)
                if there(t - 3):
                    act.wait_ge(s["lg_ps"], t - 2)
                    act.copy(lg[:, ds((t - 3) * NE, NE)], ps[3][:, 0:NE]).then_inc(s["lg"], 1)

            def pe_route(pe, t, u, i):
                if there(t):
                    pe.wait_ge(s["oT"], t + 1)
                    wait(pe, s["x_conv"], t - 1)
                    for c in range(KT):
                        mm = pe.transpose(ps[u][:, c * P:(c + 1) * P], oT[u][:, c * P:(c + 1) * P], ident)
                    mm.then_inc(s["o_ps"], 1)
                if there(t - 2):
                    front_transpose(pe, f, t - 2, u, ps[2])
                if there(t - 3):
                    pe.wait_ge(f.xnT, f.base + t - 2)
                    wait(pe, s["lg"], t - 3)
                    for c in range(KT):
                        mm = pe.matmul(ps[3][:, 0:NE], xnT[:, (1 - u) * D + c * P:(1 - u) * D + (c + 1) * P],
                                       rw3[:, c, :], start=(c == 0), stop=(c == KT - 1))
                    mm.then_inc(s["lg_ps"], 1)

            def dve_route(dve, t, u, i):
                if there(t):
                    dve.wait_ge(s["o_ps"], t + 1)
                    dve.tensor_tensor(tile_of(x, t), tile_of(x, t), ps[u][:, 0:D],
                                      ALU.add).then_inc(s["x_conv"], 1)
                    front_stats(dve, f, t, u)
                if there(t - 1):
                    front_xn(dve, f, t - 1, 1 - u, [(s["kept"], 2 * (t - 2))])

            def pool_route(pool, t, u, i):
                if there(t):
                    front_rstd(pool, f, t, u)
                if there(t - 2):
                    pool.wait_ge(f.xnT, f.base + t - 1)
                    pool.tensor_copy(tile_of(xn_all, t - 2), slot2(xn, u, D)).then_inc(s["kept"], 1)
                    pool.tensor_copy(xnT_all3[:, :, ds((t - 2) * P, P)], kt_x(slot2(xnT, u, D), P)
                                     ).then_inc(s["kept"], 1)

            def dve_positions(dve):
                n = [0]
                def step(ins):
                    n[0] += 1
                    ins.then_inc(s["route"], 1)
                    dve.wait_ge(s["route"], n[0])
                bc = lambda ap: ap.unsqueeze(2).broadcast_to([P, NB, NE])
                rows = lambda ap, k: ap.unsqueeze(1).broadcast_to([P, k, NE])
                dve.wait_ge(s["lg"], NB)
                step(dve.tensor_reduce(mx, te(lg), AX.X, ALU.max))
                step(dve.tensor_tensor(te(eq), te(lg), bc(mx), ALU.is_equal))
                step(dve.tensor_tensor(te(pr), te(eq), rows(prefer, NB), ALU.mult))
                step(dve.tensor_reduce(m2, te(pr), AX.X, ALU.max))
                dve.tensor_tensor(te(onehot), te(pr), bc(m2), ALU.is_equal).then_inc(s["rank"], 1)
                dve.wait_ge(s["gate_exp"], 1)
                step(dve.tensor_scalar(gate_e, gate_e, 1.0, None, ALU.add))
                step(dve.reciprocal(gate, gate_e))
                dve.wait_ge(s["count"], 1)
                step(dve.tensor_scalar(slots_of, COUNT, 1.0 / P, (P - 1.0) / P - 0.5 + 0.5 / P,
                                       ALU.mult, ALU.add))
                step(dve.tensor_scalar(slots_of, slots_of, MAGIC, MAGIC, ALU.add, ALU.subtract))
                step(dve.tensor_tensor(te(slot_prod), rows(slots_of, NE), te(lower), ALU.mult))
                step(dve.tensor_reduce(first_slot, te(slot_prod), AX.X, ALU.add))
                step(dve.tensor_scalar(first_row, first_slot, float(P), None, ALU.mult))
                step(dve.tensor_tensor(te(val), te(RANK), rows(first_row, NB), ALU.add))
                step(dve.tensor_tensor(te(val), te(val), te(onehot), ALU.mult))
                step(dve.tensor_reduce(posf, te(val), AX.X, ALU.add))
                dve.tensor_copy(pos, posf).then_inc(s["pos"], 1)
                step(dve.tensor_tensor(te(cmp), slot_no.unsqueeze(2).broadcast_to([P, NS, NE]),
                                       rows(first_slot, NS), ALU.is_ge))
                step(dve.tensor_reduce(esum, te(cmp), AX.X, ALU.add))
                dve.tensor_scalar(expert_of, esum, -1.0, None, ALU.add).then_inc(s["expert"], 1)

            def pe_positions(pe):
                pe.wait_ge(bf_ready, 3)
                pe.wait_ge(s["rank"], 1)
                mm = pe.matmul(RANK, tri_bf, onehot, start=True, stop=False)
                for k in range(1, NB):
                    mm = pe.matmul(RANK[:, k * NE:], ones_bf, onehot[:, 0:(NB - k) * NE],
                                   start=False, stop=(k == NB - 1))
                for k in range(NB):
                    mm = pe.matmul(COUNT, ones_bf, onehot[:, k * NE:(k + 1) * NE], start=(k == 0),
                                   stop=(k == NB - 1))
                mm.then_inc(s["count"], 1)

            def pe_shared(pe, n):
                if n < 4:
                    for c in range(2):
                        for k in range(2):
                            wait(pe, [s["sh_silu"], s["sh_h"]][k], 2 * n + c - 1)
                            for kt in range(KT):
                                mm = pe.matmul(ps[2 * c + k], w_sh_gu[:, kt, k * D + c * P:k * D + (c + 1) * P],
                                               xnT_all3[:, kt, n * 512:(n + 1) * 512],
                                               start=(kt == 0), stop=(kt == KT - 1))
                            mm.then_inc(s[f"sh_{'gu'[k]}{c}"], 1)
                if n >= 1:
                    pe.wait_ge(s["sh_h"], 2 * n)
                    for j in range(4):
                        wait(pe, s["x_shared"], 4 * (n - 1) + j - 1)
                        for c in range(KT):
                            mm = pe.matmul(ps[6 + j % 2][:, 0:D], sh_h[(n - 1) % 2][:, c, j * P:(j + 1) * P],
                                           w_sh_d[:, c, :], start=(c == 0), stop=(c == KT - 1))
                        mm.then_inc(s["sh_y"], 1)

            def act_shared(act, n):
                for c in range(2):
                    act.wait_ge(s[f"sh_g{c}"], n + 1)
                    wait(act, s["sh_h"], 2 * n + c - 1)
                    act.activation(sh_silu[c], ps[2 * c], ACT.Silu).then_inc(s["sh_silu"], 1)

            def dve_shared(dve, n):
                if n < 4:
                    for c in range(2):
                        dve.wait_ge(s[f"sh_u{c}"], n + 1)
                        dve.wait_ge(s["sh_silu"], 2 * n + c + 1)
                        wait(dve, s["sh_y"], 4 * (n - 1))
                        dve.tensor_tensor(sh_h[n % 2][:, c, :], sh_silu[c], ps[2 * c + 1],
                                          ALU.mult).then_inc(s["sh_h"], 1)
                if n >= 1:
                    for j in range(4):
                        t = 4 * (n - 1) + j
                        dve.wait_ge(s["sh_y"], t + 1)
                        dve.tensor_tensor(tile_of(x, t), tile_of(x, t), ps[6 + j % 2][:, 0:D],
                                          ALU.add).then_inc(s["x_shared"], 1)

            def slots(eng, body, ahead, behind):
                first, last = 4, (NS - ahead) - (NS - ahead) % 2
                for t in range(first):
                    body(eng, t, t % 2, t // 2)
                with eng.Fori(first // 2, last // 2) as i:
                    for u in range(2):
                        body(eng, 2 * i + u, u, i)
                for t in range(last, NS + behind):
                    body(eng, t, t % 2, t // 2)

            in_range = lambda t: not isinstance(t, int) or 0 <= t < NS

            def load_slot(sp, t, u):
                wait(sp, s["xsT_ps"], t - 1)
                sp.dma_start(xs[u], sorted_x[ds(t * P, P), :]).then_inc(s[f"xs{u}"], 16)

            def pe_turn_slot(pe, t, u, i):
                pe.wait_ge(s[f"xs{u}"], 16 * (i + 1))
                wait(pe, s["xsT"], t)
                for c in range(KT):
                    mm = pe.transpose(ps[4][:, c * P:(c + 1) * P], xs[u][:, c * P:(c + 1) * P], ident)
                mm.then_inc(s["xsT_ps"], 1)

            def pe_slot(pe, t, u, i):
                if in_range(t):
                    expert = pe.value_load(expert_of[0:1, ds(t, 1)], min_val=0, max_val=NE - 1)
                if in_range(t + 1):
                    pe_turn_slot(pe, t + 1, 1 - u, i + u)
                if in_range(t):
                    pe.wait_ge(s["xsT"], t + 1)
                    wait(pe, s["silu"], t - 1)
                    wait(pe, s["h"], t - 1)
                    for k in range(2):
                        for c in range(KT):
                            mm = pe.matmul(ps[2 * k + u][:, 0:NI], xsT[u][:, c * P:(c + 1) * P],
                                           w_ex_gu[:, c, ds(expert * (2 * NI) + k * NI, NI)],
                                           start=(c == 0), stop=(c == KT - 1))
                    mm.then_inc(s["gu"], 1)
                if in_range(t - 1):
                    pe.wait_ge(s["h"], t)
                    wait(pe, s["hT"], t - 1)
                    for c in range(KT):
                        mm = pe.transpose(ps[5][:, c * P:(c + 1) * P], h[1 - u][:, c * P:(c + 1) * P], ident)
                    mm.then_inc(s["hT_ps"], 1)
                    expert_y = pe.value_load(expert_of[0:1, ds(t - 1, 1)], min_val=0, max_val=NE - 1)
                    pe.wait_ge(s["hT"], t)
                    wait(pe, s["y"], t - 2)
                    for c in range(KT):
                        mm = pe.matmul(ps[6 + 1 - u][:, 0:D], hT[1 - u][:, c * P:(c + 1) * P],
                                       w_ex_d[:, c, ds(expert_y * D, D)], start=(c == 0),
                                       stop=(c == KT - 1))
                    mm.then_inc(s["y_ps"], 1)

            def act_turn(act, t, u):
                act.wait_ge(s["xsT_ps"], t + 1)
                wait(act, s["gu"], t - 1)
                act.copy(xsT[u], ps[4][:, 0:D]).then_inc(s["xsT"], 1)

            def act_slot(act, t, u, i):
                if in_range(t + 1):
                    act_turn(act, t + 1, 1 - u)
                if in_range(t):
                    act.wait_ge(s["gu"], t + 1)
                    wait(act, s["h"], t - 1)
                    act.activation(silu[u], ps[u][:, 0:NI], ACT.Silu).then_inc(s["silu"], 1)
                if in_range(t - 1):
                    act.wait_ge(s["hT_ps"], t)
                    wait(act, s["y_ps"], t - 2)
                    act.copy(hT[1 - u], ps[5][:, 0:D]).then_inc(s["hT"], 1)

            def dve_slot(dve, t, u, i):
                if in_range(t):
                    dve.wait_ge(s["silu"], t + 1)
                    wait(dve, s["hT_ps"], t - 1)
                    dve.tensor_tensor(h[u], silu[u], ps[2 + u][:, 0:NI], ALU.mult).then_inc(s["h"], 1)
                if in_range(t - 1):
                    dve.wait_ge(s["y_ps"], t)
                    if not isinstance(t, int) or t - 3 >= 0:
                        dve.wait_ge(s[f"stored{1 - u}"], 16 * (i - 1 + u))
                    dve.tensor_copy(y[1 - u], ps[6 + 1 - u][:, 0:D]).then_inc(s["y"], 1)

            def pool_slot(pool, t, u, i):
                if in_range(t):
                    pool.wait_ge(s["y"], t + 1)
                    pool.dma_start(sorted_y[ds(t * P, P), :], y[u]).then_inc(s[f"stored{u}"], 16)

            def pool_zero(pool):
                pool.memset(zeros, 0.0).then_inc(s["zero"], 1)
                pool.wait_ge(s["zero"], 1)
                pool.dma_start(sorted_x.rearrange("(s p) d -> p s d", p=P),
                               zeros.unsqueeze(1).broadcast_to([P, NS, D])).then_inc(s["zeroed"], 16)

            def gpsimd(pool):
                pool.wait_ge(conv_done, 66)
                pipeline(pool, lambda t, u, i: pool_route(pool, t, u, i), 0, 2)
                pool.wait_ge(s["zeroed"], 16)
                pool.wait_ge(s["pos"], 1)
                pool.wait_ge(s["kept"], 2 * NB)
                for t in range(NB):
                    pool.indirect_dma_start(out=sorted_x, out_offset=bass.IndirectOffsetOnAxis(
                        ap=pos[:, t:t + 1], axis=0), in_=tile_of(xn_all, t), in_offset=None
                        ).then_inc(s["scattered"], 16)
                slots(pool, pool_slot, 0, 0)
                pool.wait_ge(s["x_shared"], NB)
                for u in range(2):
                    pool.wait_ge(s[f"stored{u}"], 16 * NS // 2)
                for t in range(NB):
                    pool.indirect_dma_start(out=tile_of(returned, t), out_offset=None, in_=sorted_y,
                                            in_offset=bass.IndirectOffsetOnAxis(
                                                ap=pos[:, t:t + 1], axis=0)
                                            ).then_inc(gathered[t // 4], 16)

            def sync(sp):
                sp.wait_ge(s["scattered"], 16 * NB)
                for t in range(2):
                    load_slot(sp, t, t)
                with sp.Fori(1, NS // 2) as i:
                    for u in range(2):
                        load_slot(sp, 2 * i + u, u)

            def tensor(pe):
                pe.wait_ge(conv_done, 66)
                pipeline(pe, lambda t, u, i: pe_route(pe, t, u, i), 0, 3)
                pe_positions(pe)
                pe.wait_ge(moe_loaded, 64)
                pe.wait_ge(s["kept"], 2 * NB)
                for n in range(5):
                    pe_shared(pe, n)
                pe.wait_ge(s["expert"], 1)
                pe.wait_ge(s["sh_h"], 8)
                pe.wait_ge(s["x_shared"], NB)
                pe_turn_slot(pe, 0, 0, 0)
                slots(pe, pe_slot, 1, 1)

            def scalar(act):
                act.wait_ge(conv_done, 66)
                pipeline(act, lambda t, u, i: act_route(act, t, u, i), 0, 3)
                act.wait_ge(s["rank"], 1)
                act.activation(gate_e, mx, ACT.Exp, scale=-1.0).then_inc(s["gate_exp"], 1)
                for n in range(4):
                    act_shared(act, n)
                act_turn(act, 0, 0)
                slots(act, act_slot, 1, 1)

            def vector(dve):
                pipeline(dve, lambda t, u, i: dve_route(dve, t, u, i), 0, 1)
                dve_positions(dve)
                for n in range(5):
                    dve_shared(dve, n)
                slots(dve, dve_slot, 0, 1)
                for t in range(NB):
                    dve.wait_ge(gathered[t // 4], 64)
                    dve.scalar_tensor_tensor(tile_of(x, t), tile_of(returned, t), gate[:, t:t + 1],
                                             tile_of(x, t), ALU.mult, ALU.add).then_inc(s["x_new"], 1)

            return Stage(sync=sync, tensor=tensor, scalar=scalar, vector=vector,
                                   gpsimd=gpsimd, pool_zero=pool_zero, scattered=s["scattered"],
                                   zeroed=s["zeroed"],
                                   x_ready=lambda eng, t: wait(eng, s["x_new"], t + 1))

        def memory_attention(x_ready, before):
            f = Front(4, x_ready)
            s = {k: sem(f"mem_{k}") for k in (
                "mask_loaded", "mask", "s_ps", "masked", "nmax", "exp", "pT_ps", "pT", "r_ps",
                "inv", "scale", "x_new")}
            mask32 = work[:, 0:512].bitcast(I32)
            mask8 = mask32.bitcast(U8)
            bias = work[:, 512:512 + NB * P]
            o = 512 + NB * P
            sc = [work[:, o + u * P:o + (u + 1) * P] for u in range(2)]
            prob = [work[:, o + (2 + u) * P:o + (3 + u) * P] for u in range(2)]
            probT = [work[:, o + (4 + u) * P:o + (5 + u) * P] for u in range(2)]
            o += 6 * P
            valid = work[:, o:o + NB]
            cols = work[:, o + NB:o + NB + 16]
            nmax, esum, inv, scale = (lambda u: cols[:, u:u + 1]), (lambda u: cols[:, 2 + u:3 + u]), \
                (lambda u: cols[:, 4 + u:5 + u]), (lambda u: cols[:, 6 + u:7 + u])

            def sync(sp):
                before(sp)
                sp.dma_start(mask32, a["mask"].broadcast_to([P, NB * P // 4])
                             ).then_inc(s["mask_loaded"], 16)

            def pe_body(pe, t, u, i):
                if there(t):
                    front_transpose(pe, f, t, u, ps[0])
                if there(t - 2):
                    pe.wait_ge(s["exp"], t - 1)
                    wait(pe, s["pT"], t - 2)
                    pe.transpose(ps[3][:, 0:P], prob[u], ident).then_inc(s["pT_ps"], 1)
                if there(t - 1):
                    pe.wait_ge(f.xnT, f.base + t)
                    wait(pe, s["masked"], t - 2)
                    for c in range(KT):
                        mm = pe.matmul(ps[1 + 1 - u][:, 0:P], xnT[:, (1 - u) * D + c * P:(1 - u) * D + (c + 1) * P],
                                       ctxT3[:, c, ds((t - 1) * P, P)], start=(c == 0), stop=(c == KT - 1))
                    mm.then_inc(s["s_ps"], 1)
                if there(t - 2):
                    pe.wait_ge(s["pT"], t - 1)
                    wait(pe, s["x_new"], t - 3)
                    pe.matmul(ps[4 + u][:, 0:D], probT[u], tile_of(ctx_sb, t - 2), start=True,
                              stop=True).then_inc(s["r_ps"], 1)

            def act_body(act, t, u, i):
                if there(t):
                    front_copy(act, f, t, u, ps[0], s["s_ps"], t - 1)
                if there(t - 2):
                    act.wait_ge(s["pT_ps"], t - 1)
                    wait(act, s["r_ps"], t - 3)
                    act.copy(probT[u], ps[3][:, 0:P]).then_inc(s["pT"], 1)
                if there(t - 1):
                    act.wait_ge(s["nmax"], t)
                    wait(act, s["pT_ps"], t - 2)
                    wait(act, s["inv"], t - 2)
                    act.activation(prob[1 - u], sc[1 - u], ACT.Exp, bias=nmax(1 - u),
                                   accum_out=esum(1 - u)).then_inc(s["exp"], 1)

            def dve_body(dve, t, u, i):
                if there(t + 1):
                    front_stats(dve, f, t + 1, 1 - u)
                if there(t - 1):
                    dve.wait_ge(s["s_ps"], t)
                    wait(dve, s["exp"], t - 2)
                    dve.scalar_tensor_tensor(sc[1 - u], ps[1 + 1 - u][:, 0:P], float(D) ** -0.5,
                                             bias[:, ds((t - 1) * P, P)], ALU.mult, ALU.add
                                             ).then_inc(s["masked"], 1)
                    dve.wait_ge(s["masked"], t)
                    dve.tensor_reduce(nmax(1 - u), sc[1 - u], AX.X, ALU.max, negate=True
                                      ).then_inc(s["nmax"], 1)
                if there(t + 1):
                    front_xn(dve, f, t + 1, 1 - u)
                if there(t - 2):
                    dve.wait_ge(s["exp"], t - 1)
                    wait(dve, s["scale"], t - 3)
                    dve.reciprocal(inv(u), esum(u)).then_inc(s["inv"], 1)
                    dve.wait_ge(s["inv"], t - 1)
                    wait(dve, s["x_new"], t - 3)
                    dve.tensor_tensor(scale(u), inv(u), valid[:, ds(t - 2, 1)], ALU.mult
                                      ).then_inc(s["scale"], 1)
                    dve.wait_ge(s["scale"], t - 1)
                    dve.wait_ge(s["r_ps"], t - 1)
                    dve.scalar_tensor_tensor(tile_of(x, t - 2), ps[4 + u][:, 0:D], scale(u),
                                             tile_of(x, t - 2), ALU.mult, ALU.add
                                             ).then_inc(s["x_new"], 1)

            def tensor(pe):
                before(pe)
                pe.wait_ge(ctx_loaded, 32)
                pipeline(pe, lambda t, u, i: pe_body(pe, t, u, i), 0, 2)

            def scalar(act):
                before(act)
                pipeline(act, lambda t, u, i: act_body(act, t, u, i), 0, 2)

            def vector(dve):
                dve.wait_ge(s["mask_loaded"], 16)
                dve.tensor_scalar(bias, mask8, -1.0, NEG, ALU.add, ALU.mult).then_inc(s["mask"], 1)
                dve.tensor_reduce(valid, mask8.rearrange("p (b k) -> p b k", k=P), AX.X, ALU.max
                                  ).then_inc(s["mask"], 1)
                dve.wait_ge(s["mask"], 2)
                front_stats(dve, f, 0, 0)
                front_xn(dve, f, 0, 0)
                pipeline(dve, lambda t, u, i: dve_body(dve, t, u, i), 1, 2)

            def gpsimd(pool):
                pipeline(pool, lambda t, u, i: front_rstd(pool, f, t, u), 0, 0)

            return Stage(sync=sync, tensor=tensor, scalar=scalar, vector=vector,
                                   gpsimd=gpsimd, x_ready=lambda eng, t: wait(eng, s["x_new"], t + 1))

        def feed_forward(x_ready, before, scattered):
            f = Front(5, x_ready)
            f.turned = False
            s = {k: sem(f"ffn_{k}") for k in (
                "w_loaded", "rows_loaded", "w_abs", "w_tot", "w_chain", "w_done", "ones",
                "sq1", "abs1", "pow1", "r1", "col1", "q1", "int1", "qT1_ps", "qT1", "h_ps", "hb",
                "silu", "gelu", "bn2", "st2", "eps2", "rstd2", "ctr", "ln", "sq2", "abs2", "pow2",
                "r2", "col2", "q2", "int2", "qT2_ps", "qT2", "y_ps", "x_bias", "x_new")}
            w32 = [kt_x(xn_all[:, 0:2048], INNER), kt_x(xn_all[:, 2048:4096], D)]
            w32f = [xn_all[:, 0:2048], xn_all[:, 2048:4096]]
            wqf = [xnT_all[:, 0:1024].bitcast(BF16), xnT_all[:, 1024:2048].bitcast(BF16)]
            wq = [kt_x(wqf[0], INNER), kt_x(wqf[1], D)]
            rows = xn_all[:, 0:3 * INNER]
            b1, ln_g, ln_b = (rows[:, k * INNER:(k + 1) * INNER] for k in range(3))
            H = wide
            ones = small[:, 0:P]
            wc = small[:, P:P + 16]
            wabs, wtot, wmean, wscale, wk = (wc[:, 2 * k:2 * k + 2] for k in range(5))
            sq_out = work[:, 0:INNER]
            q32 = [work[:, 1024 + u * INNER:1024 + (u + 1) * INNER] for u in range(2)]
            qb = [work[:, 3072 + u * 512:3072 + (u + 1) * 512].bitcast(BF16) for u in range(2)]
            qT = [work[:, 4096 + u * 512:4096 + (u + 1) * 512].bitcast(BF16) for u in range(2)]
            cc = work[:, 5120:5120 + 64]
            col = lambda k, u: cc[:, 2 * k + u:2 * k + u + 1]
            bn2 = [work[:, 5200 + 12 * u:5212 + 12 * u] for u in range(2)]
            mv2 = [work[:, 5230 + 2 * u:5232 + 2 * u] for u in range(2)]
            inv_n = powers[:, 2:4]

            def sync(sp):
                sp.wait_ge(scattered, 16 * NB)
                cp = lambda ap: ap.rearrange("(c p) n -> p c n", p=P)
                sp.dma_start(w32[0], cp(a["ffn_w1"])).then_inc(s["w_loaded"], 16)
                sp.dma_start(w32[1], cp(a["ffn_w2"])).then_inc(s["w_loaded"], 16)
                sp.wait_ge(s["w_done"], 2)
                sp.dma_start(rows, a["ffn_rows"].partition_broadcast(P)).then_inc(s["rows_loaded"], 16)

            def dve_weights(dve):
                n = [0]
                def step(ins):
                    n[0] += 1
                    ins.then_inc(s["w_chain"], 1)
                    dve.wait_ge(s["w_chain"], n[0])
                dve.wait_ge(s["w_loaded"], 32)
                dve.memset(ones, 1.0).then_inc(s["ones"], 1)
                for k in range(2):
                    dve.tensor_reduce(wabs[:, k:k + 1], w32f[k], AX.X, ALU.add,
                                      apply_absolute_value=True).then_inc(s["w_abs"], 1)
                dve.wait_ge(s["w_tot"], 1)
                step(dve.tensor_scalar(wmean, ps[7][:, 0:2], 1.0 / (D * INNER), 1e-5, ALU.mult, ALU.max))
                step(dve.reciprocal(wscale, wmean))
                step(dve.tensor_scalar(wk, wmean, 1.0 / 127.0, None, ALU.mult))
                for k in range(2):
                    step(dve.tensor_scalar(w32f[k], w32f[k], wscale[:, k:k + 1], MAGIC, ALU.mult, ALU.add))
                    step(dve.tensor_scalar(w32f[k], w32f[k], MAGIC, 1.0, ALU.subtract, ALU.min))
                    dve.tensor_scalar(wqf[k], w32f[k], -1.0, None, ALU.max).then_inc(s["w_done"], 1)

            def pool_rms(pool, t, u, k):
                n = 3 * t
                pool.wait_ge(s[f"sq{k + 1}"], t + 1)
                pool.tensor_tensor(col(1, u), col(0, u), inv_n[:, k:k + 1], ALU.mult).then_inc(s[f"pow{k + 1}"], 1)
                pool.wait_ge(s[f"pow{k + 1}"], 2 * t + 1)
                pool.tensor_tensor(col(2, u), col(1, u), powers[:, 1:2], ALU.add).then_inc(s[f"pow{k + 1}"], 1)
                pool.wait_ge(s[f"pow{k + 1}"], 2 * t + 2)
                pool.tensor_tensor(col(3, u), col(2, u), powers[:, 0:1], ALU.pow).then_inc(s[f"r{k + 1}"], 1)

            def dve_columns(dve, t, u, k, last_scaled):
                def step(ins, c):
                    ins.then_inc(s[f"col{k + 1}"], 1)
                    dve.wait_ge(s[f"col{k + 1}"], 4 * t + c + 1)
                dve.wait_ge(s[f"r{k + 1}"], t + 1)
                wait(dve, *last_scaled)
                dve.wait_ge(s[f"abs{k + 1}"], t + 1)
                step(dve.tensor_scalar(col(5, u), col(4, u), col(3, u), 1e-5, ALU.mult, ALU.max), 0)
                step(dve.reciprocal(col(6, u), col(5, u)), 1)
                step(dve.tensor_scalar(col(7, u), col(6, u), 127.0, None, ALU.mult), 2)
                step(dve.tensor_tensor(col(8, u), col(5, u), wk[:, k:k + 1], ALU.mult), 3)

            def dve_quantise(dve, src, t, u, k, n, transposed):
                wait(dve, s[f"int{k + 1}"], t - 1)
                dve.tensor_scalar(q32[u][:, 0:n], src, col(3, u), col(7, u), ALU.mult, ALU.mult
                                  ).then_inc(s[f"q{k + 1}"], 1)
                dve.wait_ge(s[f"q{k + 1}"], t + 1)
                wait(dve, transposed, t - 1)
                dve.tensor_scalar(qb[u][:, 0:n], q32[u][:, 0:n], MAGIC, MAGIC, ALU.add, ALU.subtract
                                  ).then_inc(s[f"int{k + 1}"], 1)

            def act_first(act, t, u, i):
                if there(t):
                    act.wait_ge(f.xn, f.base + t + 1)
                    wait(act, s["sq1"], t)
                    wait(act, s["r1"], t - 1)
                    act.activation(sq_out[:, 0:D], slot2(xn, u, D), ACT.Square, accum_out=col(0, u)
                                   ).then_inc(s["sq1"], 1)
                if there(t - 2):
                    act.wait_ge(s["hb"], 2 * (t - 1))
                if there(t - 1):
                    act.wait_ge(s["qT1_ps"], t)
                    wait(act, s["h_ps"], 2 * (t - 2))
                    act.copy(qT[1 - u][:, 0:D], ps[0].bitcast(BF16)[:, 0:D]).then_inc(s["qT1"], 1)
                if there(t - 2):
                    act.activation(tile_of(H, t - 2, INNER), tile_of(H, t - 2, INNER), ACT.Silu
                                   ).then_inc(s["silu"], 1)

            def pe_first(pe, t, u, i):
                if there(t):
                    pe.wait_ge(s["int1"], t + 1)
                    wait(pe, s["qT1"], t)
                    for c in range(KT):
                        mm = pe.transpose(ps[0].bitcast(BF16)[:, c * P:(c + 1) * P],
                                          qb[u][:, c * P:(c + 1) * P], ident_bf)
                    mm.then_inc(s["qT1_ps"], 1)
                if there(t - 1):
                    pe.wait_ge(s["qT1"], t)
                    for j in range(2):
                        wait(pe, s["hb"], 2 * (t - 3) + j + 1)
                        for c in range(KT):
                            mm = pe.matmul(ps[1 + 2 * (1 - u) + j], qT[1 - u][:, c * P:(c + 1) * P],
                                           wq[0][:, c, j * 512:(j + 1) * 512], start=(c == 0),
                                           stop=(c == KT - 1))
                        mm.then_inc(s["h_ps"], 1)

            def dve_first(dve, t, u, i):
                if there(t + 1):
                    front_stats(dve, f, t + 1, 1 - u)
                if there(t):
                    dve.wait_ge(f.xn, f.base + t + 1)
                    wait(dve, s["col1"], 4 * (t - 1))
                    dve.tensor_reduce(col(4, u), slot2(xn, u, D), AX.X, ALU.max,
                                      apply_absolute_value=True).then_inc(s["abs1"], 1)
                    dve_columns(dve, t, u, 0, (s["hb"], 2 * (t - 1)))
                    dve_quantise(dve, slot2(xn, u, D), t, u, 0, D, s["qT1_ps"])
                if there(t + 1):
                    front_xn(dve, f, t + 1, 1 - u, [(s["sq1"], t), (s["q1"], t), (s["abs1"], t)])
                if there(t - 1):
                    for j in range(2):
                        dve.wait_ge(s["h_ps"], 2 * (t - 1) + j + 1)
                        dve.scalar_tensor_tensor(
                            H[:, ds((t - 1) * INNER + j * 512, 512)], ps[1 + 2 * (1 - u) + j],
                            col(8, 1 - u), b1[:, j * 512:(j + 1) * 512], ALU.mult, ALU.add
                            ).then_inc(s["hb"], 1)

            def pe_second(pe, t, u, i):
                if there(t - 1):
                    pe.wait_ge(s["int2"], t)
                    wait(pe, s["qT2"], t - 2)
                    for c in range(8):
                        mm = pe.transpose(ps[5 + 1 - u].bitcast(BF16)[:, c * P:(c + 1) * P],
                                          qb[1 - u][:, c * P:(c + 1) * P], ident_bf)
                    mm.then_inc(s["qT2_ps"], 1)
                if there(t - 2):
                    pe.wait_ge(s["qT2"], t - 1)
                    wait(pe, s["x_new"], t - 3)
                    for c in range(8):
                        mm = pe.matmul(ps[1 + u][:, 0:D], qT[u][:, c * P:(c + 1) * P], wq[1][:, c, :],
                                       start=(c == 0), stop=(c == 7))
                    mm.then_inc(s["y_ps"], 1)

            def dve_second(dve, t, u, i):
                Ht = lambda k: tile_of(H, k, INNER)
                if there(t):
                    dve.wait_ge(s["gelu"], t + 1)
                    for j in range(2):
                        dve.bn_stats(bn2[u][:, 6 * j:6 * j + 6], H[:, ds(t * INNER + j * 512, 512)]
                                     ).then_inc(s["bn2"], 1)
                    dve.wait_ge(s["bn2"], 2 * (t + 1))
                    dve.memset(tick, 0.0)
                    dve.bn_aggr(mv2[u], bn2[u]).then_inc(s["st2"], 1)
                if there(t - 2):
                    dve.wait_ge(s["y_ps"], t - 1)
                    dve.wait_ge(s["x_bias"], t - 1)
                    dve.scalar_tensor_tensor(tile_of(x, t - 2), ps[1 + u][:, 0:D], col(8, u),
                                             tile_of(x, t - 2), ALU.mult, ALU.add
                                             ).then_inc(s["x_new"], 1)
                if there(t):
                    dve.wait_ge(s["st2"], t + 1)
                    dve.scalar_tensor_tensor(Ht(t), Ht(t), mv2[u][:, 0:1], ln_g, ALU.subtract, ALU.mult
                                             ).then_inc(s["ctr"], 1)
                    dve.wait_ge(s["rstd2"], t + 1)
                    dve.wait_ge(s["ctr"], t + 1)
                    dve.scalar_tensor_tensor(Ht(t), Ht(t), rstd2(u), ln_b, ALU.mult, ALU.add
                                             ).then_inc(s["ln"], 1)
                    dve.wait_ge(s["ln"], t + 1)
                    wait(dve, s["col2"], 4 * (t - 1))
                    dve.memset(tick, 0.0)
                    dve.tensor_reduce(col(4, u), Ht(t), AX.X, ALU.max, apply_absolute_value=True
                                      ).then_inc(s["abs2"], 1)
                    dve_columns(dve, t, u, 1, (s["x_new"], t - 1))
                    dve_quantise(dve, Ht(t), t, u, 1, INNER, s["qT2_ps"])

            rstd2 = lambda u: col(10, u)

            def pool_second(pool, t, u, i):
                if there(t):
                    pool.wait_ge(s["st2"], t + 1)
                    pool.tensor_tensor(col(9, u), mv2[u][:, 1:2], powers[:, 1:2], ALU.add
                                       ).then_inc(s["eps2"], 1)
                    pool.wait_ge(s["eps2"], t + 1)
                    pool.tensor_tensor(rstd2(u), col(9, u), powers[:, 0:1], ALU.pow
                                       ).then_inc(s["rstd2"], 1)
                    pool.tensor_tensor(tile_of(x, t), tile_of(x, t), row_bias[:, 2 * D:3 * D],
                                       ALU.add).then_inc(s["x_bias"], 1)
                    pool_rms(pool, t, u, 1)

            def act_gelu(act, t):
                act.activation(tile_of(H, t, INNER), tile_of(H, t, INNER), ACT.Gelu
                               ).then_inc(s["gelu"], 1)

            def act_second(act, t, u, i):
                if there(t + 1):
                    act_gelu(act, t + 1)
                if there(t):
                    act.wait_ge(s["ln"], t + 1)
                    wait(act, s["sq2"], t)
                    wait(act, s["r2"], t - 1)
                if there(t - 1):
                    act.wait_ge(s["qT2_ps"], t)
                    wait(act, s["y_ps"], t - 2)
                    act.copy(qT[1 - u], ps[5 + 1 - u].bitcast(BF16)).then_inc(s["qT2"], 1)
                if there(t):
                    act.activation(sq_out, tile_of(H, t, INNER), ACT.Square, accum_out=col(0, u)
                                   ).then_inc(s["sq2"], 1)

            def tensor(pe):
                before(pe)
                pe.wait_ge(s["ones"], 1)
                pe.wait_ge(s["w_abs"], 2)
                pe.matmul(ps[7][:, 0:2], ones, wabs, start=True, stop=True).then_inc(s["w_tot"], 1)
                pe.wait_ge(s["w_done"], 2)
                pipeline(pe, lambda t, u, i: pe_first(pe, t, u, i), 0, 1)
                pe.wait_ge(s["hb"], 2 * NB)
                pipeline(pe, lambda t, u, i: pe_second(pe, t, u, i), 0, 2)

            def scalar(act):
                before(act)
                pipeline(act, lambda t, u, i: act_first(act, t, u, i), 0, 2)
                act.wait_ge(s["silu"], NB)
                act_gelu(act, 0)
                pipeline(act, lambda t, u, i: act_second(act, t, u, i), 1, 1)

            def vector(dve):
                dve_weights(dve)
                front_stats(dve, f, 0, 0)
                front_xn(dve, f, 0, 0)
                dve.wait_ge(s["rows_loaded"], 16)
                pipeline(dve, lambda t, u, i: dve_first(dve, t, u, i), 1, 1)
                pipeline(dve, lambda t, u, i: dve_second(dve, t, u, i), 0, 2)

            def gpsimd(pool):
                def first(t, u, i):
                    if there(t):
                        front_rstd(pool, f, t, u)
                    if there(t - 1):
                        pool_rms(pool, t - 1, 1 - u, 0)
                pipeline(pool, first, 0, 1)
                pool.wait_ge(f.xn, f.base + NB)
                pipeline(pool, lambda t, u, i: pool_second(pool, t, u, i), 0, 0)

            return Stage(sync=sync, tensor=tensor, scalar=scalar, vector=vector,
                                   gpsimd=gpsimd, x_ready=lambda eng, t: wait(eng, s["x_new"], t + 1))

        N_CONST = 8
        N_ATTN = [2, 1]
        hank_stored = sem("hank_stored")
        hank_ready = sem("hank_ready")

        def sync_loads(sp):
            v3 = lambda ap: ap.rearrange("b p d -> p b d")
            x3 = x.rearrange("p (b d) -> p b d", d=D)
            sp.dma_start(x3[:, 0:FIRST, :], v3(a["x"])[:, 0:FIRST, :]).then_inc(x_loaded0, 16)
            for dst, src in ((ident, a["ident"]), (tri, a["tri"]),
                             (of_head, a["of_head"]), (qk_cols, a["bias_cols"]),
                             (slot_iota, a["slot_iota"]), (powers, a["powers"])):
                sp.dma_start(dst, src).then_inc(const_loaded, 16)
            sp.dma_start(row_bias, a["row_bias"].partition_broadcast(P)).then_inc(const_loaded, 16)
            sp.dma_start(rw3, a["router"].rearrange("(c p) n -> p c n", p=P)).then_inc(const_loaded, 16)
            cp = lambda ap: ap.rearrange("(c p) n -> p c n", p=P)
            sp.dma_start(w_qkv3[0], cp(a["w_qkv0"])).then_inc(attn_loaded[0], 16)
            sp.dma_start(x3[:, FIRST:, :], v3(a["x"])[:, FIRST:, :]).then_inc(x_loaded1, 16)
            sp.dma_start(w_o3, cp(a["w_o"])).then_inc(attn_loaded[0], 16)
            sp.dma_start(ctxR3, cp(a["ctx_rev_t"])).then_inc(conv_loaded, 16)
            if True:
                sp.dma_start(w_sh_gu, cp(a["shared_gu"])).then_inc(moe_loaded, 16)
                sp.dma_start(w_sh_d, cp(a["shared_d"])).then_inc(moe_loaded, 16)
                sp.dma_start(w_ex_gu, cp(a["expert_gu"])).then_inc(moe_loaded, 16)
                sp.dma_start(w_ex_d, cp(a["expert_d"])).then_inc(moe_loaded, 16)
            sp.dma_start(w_qkv3[1], cp(a["w_qkv1"])).then_inc(attn_loaded[1], 16)
            sp.dma_start(kt_x(ctx_sb, D), v3(a["ctx"])).then_inc(ctx_loaded, 16)
            sp.dma_start(ctxT3, cp(a["ctx_t"])).then_inc(ctx_loaded, 16)

        ker = small[0:CH, 0:2 * D]
        ker_loaded, ker_zero = sem("ker_loaded"), sem("ker_zero")

        def pool_hank(pool):
            pool.memset(ker, 0.0).then_inc(ker_zero, 1)
            pool.wait_ge(ker_zero, 1)
            pool.dma_start(ker[:, D - 1:2 * D - 1], a["ssm"]).then_inc(ker_loaded, 16)
            pool.dma_start(small[0:CH, 2 * D:2 * D + 1], a["ssm_d"]).then_inc(ker_loaded, 16)
            pool.wait_ge(ker_loaded, 32)
            pool.tensor_tensor(ker[:, D - 1:D], ker[:, D - 1:D], small[0:CH, 2 * D:2 * D + 1],
                               ALU.add).then_inc(hank_ready, 1)
            pool.wait_ge(hank_ready, 1)
            pool.dma_start(hank, ker).then_inc(hank_stored, 16)

        def x0_ready(eng, t):
            eng.wait_ge(x_loaded0, 16)
            if not isinstance(t, int) or t >= FIRST:
                eng.wait_ge(x_loaded1, 16)

        def after(stage):
            return lambda eng: stage.x_ready(eng, NB - 1)

        nothing = lambda eng: None
        attn0 = attention(0, x0_ready, nothing)
        conv = convolution(attn0.x_ready, after(attn0))
        moe = experts(conv.summed)
        attn1 = attention(1, moe.x_ready, after(moe))
        memory = memory_attention(attn1.x_ready, after(attn1))
        ffn = feed_forward(memory.x_ready, after(memory), moe.scattered)
        every = [attn0, conv, moe, attn1, memory, ffn][:stages]

        @block.sync
        def _(sp):
            sync_loads(sp)
            for stage in every:
                if stage not in (attn0, attn1):
                    stage.sync(sp)
            if stages == 2:
                sp.wait_ge(conv.summed, 66)
            else:
                every[-1].x_ready(sp, NB - 1)
            sp.dma_start(out.rearrange("b p d -> p b d"), kt_x(outT if stages == 2 else x, D)
                         ).then_inc(out_stored, 16)
            sp.wait_ge(out_stored, 16)

        @block.gpsimd
        def _(pool):
            moe.pool_zero(pool)
            pool_hank(pool)
            for stage in every:
                stage.gpsimd(pool)
            pool.wait_ge(moe.zeroed, 16)

        @block.scalar
        def _(act):
            for stage in every:
                stage.scalar(act)

        @block.vector
        def _(dve):
            dve.wait_ge(const_loaded, 16 * N_CONST)
            dve.tensor_copy(ident_bf, ident).then_inc(bf_ready, 1)
            dve.tensor_copy(tri_bf, tri).then_inc(bf_ready, 1)
            dve.memset(ones_bf, 1.0).then_inc(bf_ready, 1)
            for stage in every:
                stage.vector(dve)

        @block.tensor
        def _(pe):
            for stage in every:
                stage.tensor(pe)


def layouts(v):
    import numpy as np
    f = {k: np.asarray(w) for k, w in v.items()}
    cols = lambda b: b.reshape(-1, P).T
    ctx = f["ctx_2048"]
    ctx_t = ctx.reshape(NB * P, D).T
    eye = np.eye(P, dtype=np.float32)
    m = {
        "x": f["x"], "ctx": ctx, "ctx_t": ctx_t, "ctx_rev_t": ctx_t[::-1],
        "w_qkv0": f["L0_attn_w_qkv"].T, "w_o": f["L0_attn_w_o"].T,
        "w_qkv1": np.concatenate([f["L1_attn_Wq"], f["L1_attn_Wk"], f["L1_attn_Wv"]], 1),
        "bias_cols": np.concatenate([cols(f["L0_attn_b_qkv"]), cols(f["L1_attn_bq"]),
                                     cols(f["L1_attn_bk"]), cols(f["L1_attn_bv"])], 1),
        "row_bias": np.concatenate([f["L0_attn_b_o"], f["L1_attn_bv"], f["L1_ffn_b2"]]),
        "ssm": f["L0_xattn_ssm_kernel"], "ssm_d": f["L0_xattn_D"].reshape(-1, 1),
        "router": f["L0_ffn_router_w"].T,
        "shared_gu": np.concatenate([f["L0_ffn_shared_gate"].T, f["L0_ffn_shared_up"].T], 1),
        "shared_d": f["L0_ffn_shared_down"].T,
        "expert_gu": np.concatenate([f["L0_ffn_w1"], f["L0_ffn_v1"]], 2).transpose(1, 0, 2).reshape(D, -1),
        "expert_d": f["L0_ffn_w2"].transpose(1, 0, 2).reshape(NI, -1),
        "mask": f["mask_BxS2_bk0"].reshape(1, -1).view(np.int32),
        "ffn_w1": f["L1_ffn_w1"].T, "ffn_w2": f["L1_ffn_w2"].T,
        "ffn_rows": np.concatenate([f["L1_ffn_b1"], f["L1_ffn_ln_g"], f["L1_ffn_ln_b"]]),
        "ident": eye,
        "tri": np.triu(np.ones((P, P), np.float32), 1),
        "of_head": np.stack([(np.arange(P) // HD) % GH == e for e in range(GH)], 1).astype(np.float32),
        "powers": np.tile(np.float32([-0.5, EPS, 1 / D, 1 / INNER]), (P, 1)),
        "slot_iota": np.tile(np.concatenate([np.arange(NS), NE - np.arange(NE),
                                             np.tril(np.ones((NE, NE)), -1).ravel()]), (P, 1)).astype(np.float32),
    }
    return {k: np.ascontiguousarray(w) for k, w in m.items()}


def kernel(**inputs):
    import numpy as np
    import concourse.bacc as bacc
    from concourse.bass_utils import run_bass_kernel_spmd
    nc = bacc.Bacc("TRN2", target_bir_lowering=False, num_devices=1)
    arrays = layouts(inputs)
    a = {k: nc.dram_tensor("in_" + k, w.shape, mybir.dt.from_np(w.dtype), kind="ExternalInput").ap()
         for k, w in arrays.items()}
    out = nc.dram_tensor("out_x", (NB, P, D), F32, kind="ExternalOutput").ap()
    build(nc, a, out)
    r = run_bass_kernel_spmd(nc, [{"in_" + k: w for k, w in arrays.items()}], core_ids=[0])
    return r.results[0]["out_x"]
```
